# Optimizing a Trainium2 kernel written in Bass

```python
import numpy as np
import jax
import jax.numpy as jnp

def _softmax(x, axis=-1):
    return jax.nn.softmax(x, axis=axis)

def _gelu(x):
    return jax.nn.gelu(x, approximate=True)

def _silu(x):
    return jax.nn.silu(x)

def _sigmoid(x):
    return jax.nn.sigmoid(x)

def _layernorm(x, axis=-1, eps=1e-05):
    m = jnp.mean(x, axis=axis, keepdims=True)
    v = jnp.var(x, axis=axis, keepdims=True)
    return (x - m) / jnp.sqrt(v + eps)

def _scatter_add(tgt, idx, src, axis=0):
    return tgt.at[idx].add(src)

def _segment_sum(src, seg, n):
    return jax.ops.segment_sum(src, seg, n)
kernel_name = 'mk_dlrm_tower_d1_rec_r8_f150d3'

def setup_inputs(seed: int=0):
    np.random.seed(seed)
    _w = jnp.asarray

    def _rec_inputs():
        import jax
        import jax.numpy as jnp
        _tk = jax.random.key(seed)
        dense_ctx = jax.random.normal(jax.random.fold_in(_tk, 190), (512, 16), jnp.float32)
        ids = jnp.stack([jax.random.randint(jax.random.fold_in(_tk, 200 + f), (512,), 0, v, jnp.int32) for f, v in enumerate([12500, 125000, 1250, 1000, 1250, 1000, 12500, 1250, 1250, 125000, 1250, 1000, 125000, 12500, 125000, 1250, 125000, 125000, 1000, 1000, 125000, 1000, 1250, 1250, 125000, 125000, 1250, 125000, 1250, 125000, 1250, 12500, 12500, 1250, 1000, 125000, 1250, 1250, 12500])], axis=1)
        tbl_0 = 0.05 * jax.random.normal(jax.random.fold_in(_tk, 500 + 0), (12500, 16), jnp.float32)
        tbl_1 = 0.05 * jax.random.normal(jax.random.fold_in(_tk, 500 + 1), (125000, 16), jnp.float32)
        tbl_2 = 0.05 * jax.random.normal(jax.random.fold_in(_tk, 500 + 2), (1250, 16), jnp.float32)
        tbl_3 = 0.05 * jax.random.normal(jax.random.fold_in(_tk, 500 + 3), (1000, 16), jnp.float32)
        tbl_4 = 0.05 * jax.random.normal(jax.random.fold_in(_tk, 500 + 4), (1250, 16), jnp.float32)
        tbl_5 = 0.05 * jax.random.normal(jax.random.fold_in(_tk, 500 + 5), (1000, 16), jnp.float32)
        tbl_6 = 0.05 * jax.random.normal(jax.random.fold_in(_tk, 500 + 6), (12500, 16), jnp.float32)
        tbl_7 = 0.05 * jax.random.normal(jax.random.fold_in(_tk, 500 + 7), (1250, 16), jnp.float32)
        tbl_8 = 0.05 * jax.random.normal(jax.random.fold_in(_tk, 500 + 8), (1250, 16), jnp.float32)
        tbl_9 = 0.05 * jax.random.normal(jax.random.fold_in(_tk, 500 + 9), (125000, 16), jnp.float32)
        tbl_10 = 0.05 * jax.random.normal(jax.random.fold_in(_tk, 500 + 10), (1250, 16), jnp.float32)
        tbl_11 = 0.05 * jax.random.normal(jax.random.fold_in(_tk, 500 + 11), (1000, 16), jnp.float32)
        tbl_12 = 0.05 * jax.random.normal(jax.random.fold_in(_tk, 500 + 12), (125000, 16), jnp.float32)
        tbl_13 = 0.05 * jax.random.normal(jax.random.fold_in(_tk, 500 + 13), (12500, 16), jnp.float32)
        tbl_14 = 0.05 * jax.random.normal(jax.random.fold_in(_tk, 500 + 14), (125000, 16), jnp.float32)
        tbl_15 = 0.05 * jax.random.normal(jax.random.fold_in(_tk, 500 + 15), (1250, 16), jnp.float32)
        tbl_16 = 0.05 * jax.random.normal(jax.random.fold_in(_tk, 500 + 16), (125000, 16), jnp.float32)
        tbl_17 = 0.05 * jax.random.normal(jax.random.fold_in(_tk, 500 + 17), (125000, 16), jnp.float32)
        tbl_18 = 0.05 * jax.random.normal(jax.random.fold_in(_tk, 500 + 18), (1000, 16), jnp.float32)
        tbl_19 = 0.05 * jax.random.normal(jax.random.fold_in(_tk, 500 + 19), (1000, 16), jnp.float32)
        tbl_20 = 0.05 * jax.random.normal(jax.random.fold_in(_tk, 500 + 20), (125000, 16), jnp.float32)
        tbl_21 = 0.05 * jax.random.normal(jax.random.fold_in(_tk, 500 + 21), (1000, 16), jnp.float32)
        tbl_22 = 0.05 * jax.random.normal(jax.random.fold_in(_tk, 500 + 22), (1250, 16), jnp.float32)
        tbl_23 = 0.05 * jax.random.normal(jax.random.fold_in(_tk, 500 + 23), (1250, 16), jnp.float32)
        tbl_24 = 0.05 * jax.random.normal(jax.random.fold_in(_tk, 500 + 24), (125000, 16), jnp.float32)
        tbl_25 = 0.05 * jax.random.normal(jax.random.fold_in(_tk, 500 + 25), (125000, 16), jnp.float32)
        tbl_26 = 0.05 * jax.random.normal(jax.random.fold_in(_tk, 500 + 26), (1250, 16), jnp.float32)
        tbl_27 = 0.05 * jax.random.normal(jax.random.fold_in(_tk, 500 + 27), (125000, 16), jnp.float32)
        tbl_28 = 0.05 * jax.random.normal(jax.random.fold_in(_tk, 500 + 28), (1250, 16), jnp.float32)
        tbl_29 = 0.05 * jax.random.normal(jax.random.fold_in(_tk, 500 + 29), (125000, 16), jnp.float32)
        tbl_30 = 0.05 * jax.random.normal(jax.random.fold_in(_tk, 500 + 30), (1250, 16), jnp.float32)
        tbl_31 = 0.05 * jax.random.normal(jax.random.fold_in(_tk, 500 + 31), (12500, 16), jnp.float32)
        tbl_32 = 0.05 * jax.random.normal(jax.random.fold_in(_tk, 500 + 32), (12500, 16), jnp.float32)
        tbl_33 = 0.05 * jax.random.normal(jax.random.fold_in(_tk, 500 + 33), (1250, 16), jnp.float32)
        tbl_34 = 0.05 * jax.random.normal(jax.random.fold_in(_tk, 500 + 34), (1000, 16), jnp.float32)
        tbl_35 = 0.05 * jax.random.normal(jax.random.fold_in(_tk, 500 + 35), (125000, 16), jnp.float32)
        tbl_36 = 0.05 * jax.random.normal(jax.random.fold_in(_tk, 500 + 36), (1250, 16), jnp.float32)
        tbl_37 = 0.05 * jax.random.normal(jax.random.fold_in(_tk, 500 + 37), (1250, 16), jnp.float32)
        tbl_38 = 0.05 * jax.random.normal(jax.random.fold_in(_tk, 500 + 38), (12500, 16), jnp.float32)
        _rk = jax.random.fold_in(_tk, 7)
        W_top1 = 0.0606339 * jax.random.normal(jax.random.fold_in(_tk, 801), (272, 512), jnp.float32)
        W_top2 = 0.0441942 * jax.random.normal(jax.random.fold_in(_tk, 802), (512, 256), jnp.float32)
        W_top3 = 0.0625 * jax.random.normal(jax.random.fold_in(_tk, 803), (256, 1), jnp.float32)
        b_top1 = jnp.zeros((512,), jnp.float32)
        b_top2 = jnp.zeros((256,), jnp.float32)
        return (dense_ctx, ids, tbl_0, tbl_1, tbl_2, tbl_3, tbl_4, tbl_5, tbl_6, tbl_7, tbl_8, tbl_9, tbl_10, tbl_11, tbl_12, tbl_13, tbl_14, tbl_15, tbl_16, tbl_17, tbl_18, tbl_19, tbl_20, tbl_21, tbl_22, tbl_23, tbl_24, tbl_25, tbl_26, tbl_27, tbl_28, tbl_29, tbl_30, tbl_31, tbl_32, tbl_33, tbl_34, tbl_35, tbl_36, tbl_37, tbl_38, W_top1, b_top1, W_top2, b_top2, W_top3)
    dense_ctx, ids, tbl_0, tbl_1, tbl_2, tbl_3, tbl_4, tbl_5, tbl_6, tbl_7, tbl_8, tbl_9, tbl_10, tbl_11, tbl_12, tbl_13, tbl_14, tbl_15, tbl_16, tbl_17, tbl_18, tbl_19, tbl_20, tbl_21, tbl_22, tbl_23, tbl_24, tbl_25, tbl_26, tbl_27, tbl_28, tbl_29, tbl_30, tbl_31, tbl_32, tbl_33, tbl_34, tbl_35, tbl_36, tbl_37, tbl_38, W_top1, b_top1, W_top2, b_top2, W_top3 = _rec_inputs()

    def _L0_rec_setup():
        import jax, jax.numpy as jnp
        import numpy as np
        LAYER_SIZES = [128, 128, 128]
        F0 = 39
        D = 16
        B = 256
        key = jax.random.key(seed)
        ks = jax.random.split(key, 4)
        field_nums = [F0, LAYER_SIZES[0] // 2, LAYER_SIZES[1] // 2]
        x = jax.random.normal(ks[0], (B, F0, D), dtype=jnp.float32)
        W0 = jax.random.normal(ks[1], (F0 * field_nums[0], LAYER_SIZES[0]), dtype=jnp.float32) * 0.05
        W1 = jax.random.normal(ks[2], (F0 * field_nums[1], LAYER_SIZES[1]), dtype=jnp.float32) * 0.05
        W2 = jax.random.normal(ks[3], (F0 * field_nums[2], LAYER_SIZES[2]), dtype=jnp.float32) * 0.05
        b0 = jnp.zeros((LAYER_SIZES[0],), jnp.float32)
        b1 = jnp.zeros((LAYER_SIZES[1],), jnp.float32)
        b2 = jnp.zeros((LAYER_SIZES[2],), jnp.float32)
        return {'x': x, 'W0': W0, 'W1': W1, 'W2': W2, 'b0': b0, 'b1': b1, 'b2': b2}
    _L0_rec_all = _L0_rec_setup()
    _L0_rec_in = {k: v for k, v in _L0_rec_all.items() if k in ('W0', 'W1', 'W2', 'b0', 'b1', 'b2')}
    del _L0_rec_all
    return {'dense_ctx': dense_ctx, 'ids': ids, 'tbl_0': tbl_0, 'tbl_1': tbl_1, 'tbl_2': tbl_2, 'tbl_3': tbl_3, 'tbl_4': tbl_4, 'tbl_5': tbl_5, 'tbl_6': tbl_6, 'tbl_7': tbl_7, 'tbl_8': tbl_8, 'tbl_9': tbl_9, 'tbl_10': tbl_10, 'tbl_11': tbl_11, 'tbl_12': tbl_12, 'tbl_13': tbl_13, 'tbl_14': tbl_14, 'tbl_15': tbl_15, 'tbl_16': tbl_16, 'tbl_17': tbl_17, 'tbl_18': tbl_18, 'tbl_19': tbl_19, 'tbl_20': tbl_20, 'tbl_21': tbl_21, 'tbl_22': tbl_22, 'tbl_23': tbl_23, 'tbl_24': tbl_24, 'tbl_25': tbl_25, 'tbl_26': tbl_26, 'tbl_27': tbl_27, 'tbl_28': tbl_28, 'tbl_29': tbl_29, 'tbl_30': tbl_30, 'tbl_31': tbl_31, 'tbl_32': tbl_32, 'tbl_33': tbl_33, 'tbl_34': tbl_34, 'tbl_35': tbl_35, 'tbl_36': tbl_36, 'tbl_37': tbl_37, 'tbl_38': tbl_38, 'W_top1': W_top1, 'b_top1': b_top1, 'W_top2': W_top2, 'b_top2': b_top2, 'W_top3': W_top3, 'L0_rec_W0': _L0_rec_in['W0'], 'L0_rec_W1': _L0_rec_in['W1'], 'L0_rec_W2': _L0_rec_in['W2'], 'L0_rec_b0': _L0_rec_in['b0'], 'L0_rec_b1': _L0_rec_in['b1'], 'L0_rec_b2': _L0_rec_in['b2']}

def reference(dense_ctx, ids, tbl_0, tbl_1, tbl_2, tbl_3, tbl_4, tbl_5, tbl_6, tbl_7, tbl_8, tbl_9, tbl_10, tbl_11, tbl_12, tbl_13, tbl_14, tbl_15, tbl_16, tbl_17, tbl_18, tbl_19, tbl_20, tbl_21, tbl_22, tbl_23, tbl_24, tbl_25, tbl_26, tbl_27, tbl_28, tbl_29, tbl_30, tbl_31, tbl_32, tbl_33, tbl_34, tbl_35, tbl_36, tbl_37, tbl_38, W_top1, b_top1, W_top2, b_top2, W_top3, L0_rec_W0, L0_rec_W1, L0_rec_W2, L0_rec_b0, L0_rec_b1, L0_rec_b2):
    import jax
    import jax.numpy as jnp

    def _L0_rec_ref(x, W0, W1, W2, b0, b1, b2):
        import jax, jax.numpy as jnp
        import numpy as np
        LAYER_SIZES = [128, 128, 128]
        F0 = 39
        D = 16
        B = 256
        Ws = [W0, W1, W2]
        bs = [b0, b1, b2]
        h = x
        outs = []
        n_layers = len(LAYER_SIZES)
        for i, S in enumerate(LAYER_SIZES):
            Fk = h.shape[1]
            Wr = Ws[i].reshape(F0, Fk, S)
            out = jax.nn.relu(jnp.einsum('bfd,bgd,fgs->bsd', x, h, Wr) + bs[i][None, :, None])
            if i != n_layers - 1:
                h, direct = (out[:, :S // 2], out[:, S // 2:])
            else:
                direct = out
            outs.append(direct)
        result = jnp.concatenate(outs, axis=1)
        return jnp.sum(result, axis=-1)
    e = jnp.stack([tbl_0[ids[:, 0]], tbl_1[ids[:, 1]], tbl_2[ids[:, 2]], tbl_3[ids[:, 3]], tbl_4[ids[:, 4]], tbl_5[ids[:, 5]], tbl_6[ids[:, 6]], tbl_7[ids[:, 7]], tbl_8[ids[:, 8]], tbl_9[ids[:, 9]], tbl_10[ids[:, 10]], tbl_11[ids[:, 11]], tbl_12[ids[:, 12]], tbl_13[ids[:, 13]], tbl_14[ids[:, 14]], tbl_15[ids[:, 15]], tbl_16[ids[:, 16]], tbl_17[ids[:, 17]], tbl_18[ids[:, 18]], tbl_19[ids[:, 19]], tbl_20[ids[:, 20]], tbl_21[ids[:, 21]], tbl_22[ids[:, 22]], tbl_23[ids[:, 23]], tbl_24[ids[:, 24]], tbl_25[ids[:, 25]], tbl_26[ids[:, 26]], tbl_27[ids[:, 27]], tbl_28[ids[:, 28]], tbl_29[ids[:, 29]], tbl_30[ids[:, 30]], tbl_31[ids[:, 31]], tbl_32[ids[:, 32]], tbl_33[ids[:, 33]], tbl_34[ids[:, 34]], tbl_35[ids[:, 35]], tbl_36[ids[:, 36]], tbl_37[ids[:, 37]], tbl_38[ids[:, 38]]], axis=1)
    z = _L0_rec_ref(e, L0_rec_W0, L0_rec_W1, L0_rec_W2, L0_rec_b0, L0_rec_b1, L0_rec_b2)
    z = z.reshape(z.shape[0], -1)
    h = jnp.concatenate([z, dense_ctx], axis=1)
    h = jnp.maximum(h @ W_top1 + b_top1, 0.0)
    h = jnp.maximum(h @ W_top2 + b_top2, 0.0)
    y = h @ W_top3
    return y

_drawn_inputs = setup_inputs


def setup_inputs(seed=0):
    import zlib

    import numpy as np

    out = dict(_drawn_inputs(seed))
    spreads = {'b_top1': (0.0, 2.0),
     'b_top2': (0.0, 2.0),
     'L0_rec_b0': (0.0, 0.374),
     'L0_rec_b1': (0.0, 0.548),
     'L0_rec_b2': (0.0, 0.8)}
    factors = {'tbl_0': 8.0,
     'tbl_1': 8.0,
     'tbl_2': 8.0,
     'tbl_3': 8.0,
     'tbl_4': 8.0,
     'tbl_5': 8.0,
     'tbl_6': 8.0,
     'tbl_7': 8.0,
     'tbl_8': 8.0,
     'tbl_9': 8.0,
     'tbl_10': 8.0,
     'tbl_11': 8.0,
     'tbl_12': 8.0,
     'tbl_13': 8.0,
     'tbl_14': 8.0,
     'tbl_15': 8.0,
     'tbl_16': 8.0,
     'tbl_17': 8.0,
     'tbl_18': 8.0,
     'tbl_19': 8.0,
     'tbl_20': 8.0,
     'tbl_21': 8.0,
     'tbl_22': 7.22,
     'tbl_23': 8.0,
     'tbl_24': 8.0,
     'tbl_25': 8.0,
     'tbl_26': 7.691,
     'tbl_27': 8.0,
     'tbl_28': 8.0,
     'tbl_29': 8.0,
     'tbl_30': 8.0,
     'tbl_31': 7.945,
     'tbl_32': 8.0,
     'tbl_33': 8.0,
     'tbl_34': 8.0,
     'tbl_35': 8.0,
     'tbl_36': 8.0,
     'tbl_37': 8.0,
     'tbl_38': 8.0,
     'L0_rec_W0': 6.595,
     'L0_rec_W1': 3.294,
     'L0_rec_W2': 2.784,
     'dense_ctx': 8.0}
    for name, (base, spread) in spreads.items():
        noise = np.random.default_rng([zlib.crc32(name.encode()), seed]).standard_normal(out[name].shape)
        drawn = base * np.exp(spread * noise) if base else spread * noise
        out[name] = jnp.asarray(drawn.astype(out[name].dtype))
    for name, factor in factors.items():
        out[name] = (out[name] * factor).astype(out[name].dtype)
    return out
```

```python
from contextlib import ExitStack

import numpy as np
import concourse.bass as bass
from concourse import mybir

F32 = mybir.dt.float32
I32 = mybir.dt.int32
ALU = mybir.AluOpType
ACT = mybir.ActivationFunctionType
AX = mybir.AxisListType

B, F, D = 512, 39, 16
S = 128
G = S // 2
CB = 32
N = CB * D
CH = B // CB
FG = 128 // CB
NG = -(-F // FG)
LAST = (F - (NG - 1) * FG) * CB
WRAP_G = 5
XROWS = F + WRAP_G * FG
R = F // 2 + 1
P0 = 3 * F
T0 = -(-R // 3)
K0_LAST = (R - 3 * (T0 - 1)) * F
T1 = -(-F // 2)
K1_LAST = (F - 2 * (T1 - 1)) * G
T1_LO = T1 // 2
GT = 4
RING = 3
H1, H2 = 512, 256
ZD = 2 * S
DC = 16

TILES = [T0, T1, T1]
KLAST = [K0_LAST, K1_LAST, K1_LAST]
GROUPS = [-(-t // GT) for t in TILES]
PER_CHUNK = sum(GROUPS)


def first_group(layer, c):
    lead = GROUPS[0] + GROUPS[1] + GROUPS[0]
    if layer == 1:
        return c * PER_CHUNK + GROUPS[0]
    if layer == 2:
        if isinstance(c, int) and c == CH - 1:
            return CH * PER_CHUNK - GROUPS[2]
        return c * PER_CHUNK + lead
    if isinstance(c, int) and c == 0:
        return 0
    return c * PER_CHUNK + lead - PER_CHUNK - GROUPS[0]


def run_steps(eng, step):
    step(0, 0, 0)
    step(1, 0, 0)
    step(0, 1, 1)
    with eng.Fori(0, CH - 2, 2) as c0:
        for u in range(2):
            step(2, c0 + u, u)
            step(1, c0 + (u + 1), (u + 1) % 2)
            step(0, c0 + (u + 2), u)
    step(2, CH - 2, 0)
    step(1, CH - 1, 1)
    step(2, CH - 1, 1)


def group_slot(layer, par, gi):
    base = first_group(layer, par + 2)
    return (base + gi) % RING


assert PER_CHUNK % RING == 0 and CH % 2 == 0


def build(nc, tables, ids, offs, dense, w0a, w0b, w1, w2, wt1, wt2, cols, out):
    with ExitStack() as ctx:
        def sb(name, shape, dt=F32):
            return ctx.enter_context(nc.sbuf_tensor(name, shape, dt))

        def psum(name, shape):
            return ctx.enter_context(nc.psum_tensor(name, shape, F32))

        def sem(name):
            return ctx.enter_context(nc.semaphore(name))

        xt = nc.dram_tensor("xt_scratch", (CH, XROWS, N), F32, kind="Internal").ap()

        ids_sb = sb("ids_sb", [128, CH * NG], I32)
        offs_sb = sb("offs_sb", [128, NG], I32)
        idx_sb = sb("idx_sb", [128, 2, NG], I32)
        gath = sb("gath", [128, 2, NG, D])
        w0_sb = sb("w0_sb", [128, T0, S])
        w0b_sb = sb("w0b_sb", [128, T0, S])
        w1_sb = sb("w1_sb", [128, T1, S])
        w2_sb = sb("w2_sb", [128, T1, S])
        w_sb = [w0_sb, w1_sb, w2_sb]
        cols_sb = sb("cols_sb", [128, 3 + H1 // 128 + 2 * (H2 // 128)])
        bias = cols_sb[:, 0:3]
        bt1_sb = cols_sb[:, 3:3 + H1 // 128]
        bt2_sb = cols_sb[:, 3 + H1 // 128:3 + (H1 + H2) // 128]
        wt3_sb = cols_sb[:, 3 + (H1 + H2) // 128:3 + (H1 + 2 * H2) // 128]
        base = sb("base", [128, 2, N])
        rot = sb("rot", [128, 2, T0, N])
        xrep = sb("xrep", [128, 2, T1, N])
        z = sb("z", [128, RING, GT, N])
        h = sb("h", [128, 2, N])
        direct = sb("direct", [128, 3, N])
        zt = sb("zt", [128, 4, B])
        wt1_sb = sb("wt1_sb", [128, 4, H1])
        wt2_sb = sb("wt2_sb", [128, H1 // 128, H2])
        m1 = z[:, 0, 0:H1 // 128, :]
        m2 = z[:, 1, 0:H2 // 128, :]
        y_sb = sb("y_sb", [1, B])

        acc = [psum(f"acc{i}", [128, N]) for i in range(3)]
        pm = [psum(f"pm{i}", [128, B]) for i in range(H1 // 128)]

        s_ids = sem("s_ids")
        s_idx = sem("s_idx")
        s_w0 = sem("s_w0")
        s_w0zero = sem("s_w0zero")
        s_w0fold = sem("s_w0fold")
        s_w = [None, sem("s_w1"), sem("s_w2")]
        s_cols = sem("s_cols")
        s_wt = sem("s_wt")
        s_gathered = [sem(f"s_gathered{i}") for i in range(2)]
        s_stored = [sem(f"s_stored{i}") for i in range(2)]
        s_rot = [sem(f"s_rot{i}") for i in range(2)]
        s_xlo = [sem(f"s_xlo{i}") for i in range(2)]
        s_xhi = [sem(f"s_xhi{i}") for i in range(2)]
        s_zready = sem("s_zready")
        s_zused = sem("s_zused")
        s_hready = [None, sem("s_hready1"), sem("s_hready2")]
        s_evac = [sem(f"s_evac{i}") for i in range(3)]
        s_summed = [sem(f"s_summed{i}") for i in range(3)]
        s_m1 = sem("s_m1")
        s_m1r = sem("s_m1r")
        s_m2 = sem("s_m2")
        s_m2r = sem("s_m2r")
        s_y = sem("s_y")
        s_yc = sem("s_yc")
        s_out = sem("s_out")

        block = ctx.enter_context(nc.Block())

        @block.gpsimd
        def _(pool):
            pool.wait_ge(s_ids, 32)
            nc.gpsimd.memset(w0b_sb[0:64, 0, :], 0.0).then_inc(s_w0zero, 1)

            def gather(c, slot):
                nc.gpsimd.tensor_tensor(idx_sb[:, slot, :], ids_sb[:, bass.ds(c * NG, NG)], offs_sb[:, :],
                                        ALU.add).then_inc(s_idx, 1)
                pool.wait_ge(s_idx, c + 1)
                pool.nop(nofuse=True)
                for j in range(NG):
                    p = 128 if j < NG - 1 else LAST
                    nc.gpsimd.indirect_dma_start(
                        gath[0:p, slot, j, :], None, tables,
                        bass.IndirectOffsetOnAxis(ap=idx_sb[0:p, slot, j:j + 1], axis=0),
                    ).then_inc(s_gathered[slot], 16)

            gather(0, 0)
            gather(1, 1)
            with pool.Fori(1, CH // 2) as i:
                for u in range(2):
                    pool.wait_ge(s_stored[u], i * 48)
                    gather(i * 2 + u, u)

        @block.sync
        def _(sp):
            sp.dma_start(ids_sb[:, :], ids).then_inc(s_ids, 16)
            sp.dma_start(offs_sb[:, :], offs).then_inc(s_ids, 16)

            def store(c, slot, n):
                sp.wait_ge(s_gathered[slot], n * (16 * NG))
                g = gath[:, slot, :, :]
                m = (NG - 1) * FG
                sp.dma_start(xt[c, 0:m, :].rearrange("(j q) (b d) -> (q b) j d", q=FG, d=D),
                             g[:, 0:NG - 1, :]).then_inc(s_stored[slot], 16)
                sp.dma_start(xt[c, m:F, :].rearrange("q (b d) -> (q b) d", d=D),
                             g[0:LAST, NG - 1, :]).then_inc(s_stored[slot], 16)
                sp.dma_start(xt[c, F:XROWS, :].rearrange("(j q) (b d) -> (q b) j d", q=FG, d=D),
                             g[:, 0:WRAP_G, :]).then_inc(s_stored[slot], 16)

            def fields(c, first, dims):
                return bass.AP(tensor=xt.tensor, offset=c * (XROWS * N) + first * N,
                               ap=[[n * N, count] for n, count in dims] + [[1, N]])

            def load_rot(c, slot):
                for j in range(3):
                    nt = (R - j + 2) // 3
                    sp.dma_start(base[j * F:(j + 1) * F, slot, :], fields(c, 0, [[1, F]])).then_inc(s_rot[slot], 16)
                    sp.dma_start(rot[j * F:(j + 1) * F, slot, 0:nt, :],
                                 fields(c, j, [[1, F], [3, nt]])).then_inc(s_rot[slot], 16)

            def load_x(c, slot, lo):
                t0, t1 = (0, T1_LO) if lo else (T1_LO, T1)
                for half in range(2):
                    tn = t1 if half == 0 or t1 < T1 else (F // 2)
                    sp.dma_start(xrep[half * G:(half + 1) * G, slot, t0:tn, :],
                                 fields(c, 2 * t0 + half, [[0, G], [2, tn - t0]])
                                 ).then_inc((s_xlo if lo else s_xhi)[slot], 16)

            store(0, 0, 1)
            store(1, 1, 1)
            sp.dma_start(w0_sb[0:P0, 0:T0 - 1, :], w0a[0:P0 * (T0 - 1), :].rearrange("(t p) s -> p t s", p=P0)
                         ).then_inc(s_w0, 16)
            sp.dma_start(w0_sb[0:K0_LAST, T0 - 1, :], w0a[P0 * (T0 - 1):, :]).then_inc(s_w0, 16)
            sp.wait_ge(s_w0zero, 1)
            sp.dma_start(w0b_sb[F:P0, 0, :], w0b[0:2 * F, :]).then_inc(s_w0, 16)
            sp.dma_start(w0b_sb[0:P0, 1:T0 - 1, :],
                         w0b[2 * F:2 * F + P0 * (T0 - 2), :].rearrange("(t p) s -> p t s", p=P0)
                         ).then_inc(s_w0, 16)
            sp.dma_start(w0b_sb[0:K0_LAST, T0 - 1, :], w0b[2 * F + P0 * (T0 - 2):, :]).then_inc(s_w0, 16)
            for l, w in ((1, w1), (2, w2)):
                full = (T1 - 1) * 128
                sp.dma_start(w_sb[l][:, 0:T1 - 1, :], w[0:full, :].rearrange("(t p) s -> p t s", p=128)
                             ).then_inc(s_w[l], 16)
                sp.dma_start(w_sb[l][0:K1_LAST, T1 - 1, :], w[full:, :]).then_inc(s_w[l], 16)
                if l == 1:
                    sp.dma_start(cols_sb[:, :], cols).then_inc(s_cols, 16)
                    for u in range(2):
                        sp.wait_ge(s_stored[u], 48)
                        load_rot(u, u)
                        load_x(u, u, True)
                        load_x(u, u, False)
            sp.dma_start(wt1_sb[G:128, 0, :], wt1[0:G, :]).then_inc(s_wt, 16)
            sp.dma_start(wt1_sb[G:128, 1, :], wt1[G:2 * G, :]).then_inc(s_wt, 16)
            sp.dma_start(wt1_sb[:, 2, :], wt1[2 * G:ZD, :]).then_inc(s_wt, 16)
            sp.dma_start(wt1_sb[0:DC, 3, :], wt1[ZD:ZD + DC, :]).then_inc(s_wt, 16)
            sp.dma_start(zt[0:DC, 3, :], dense).then_inc(s_wt, 16)
            sp.dma_start(wt2_sb[:, :, :], wt2.rearrange("(k p) n -> p k n", p=128)).then_inc(s_wt, 16)

            with sp.Fori(1, CH // 2) as i:
                for u in range(2):
                    c = i * 2 + u
                    store(c, u, i + 1)
                    sp.wait_ge(s_stored[u], i * 48 + 48)
                    sp.wait_ge(s_zready, first_group(1, c - 2))
                    load_rot(c, u)
                    sp.wait_ge(s_zready, first_group(2, c - 2) + (T1_LO - 1) // GT + 1)
                    load_x(c, u, True)
                    sp.wait_ge(s_zready, first_group(2, c - 2) + GROUPS[2])
                    load_x(c, u, False)
            sp.wait_ge(s_yc, 1)
            sp.dma_start(out.rearrange("b o -> o b"), y_sb[:, :]).then_inc(s_out, 16)
            sp.wait_ge(s_out, 16)

        @block.vector
        def _(dve):
            dve.wait_ge(s_w0zero, 1)
            dve.wait_ge(s_w0, 80)
            nc.vector.tensor_tensor(w0_sb[0:P0, 0:T0 - 1, :], w0_sb[0:P0, 0:T0 - 1, :],
                                    w0b_sb[0:P0, 0:T0 - 1, :], ALU.add).then_inc(s_w0fold, 1)
            nc.vector.tensor_tensor(w0_sb[0:K0_LAST, T0 - 1, :], w0_sb[0:K0_LAST, T0 - 1, :],
                                    w0b_sb[0:K0_LAST, T0 - 1, :], ALU.add).then_inc(s_w0fold, 1)

            def sum_over_d(layer, c, n):
                p0 = 0 if layer == 2 else G
                dve.wait_ge(s_evac[layer], n)
                nc.vector.tensor_reduce(
                    zt[p0:128, layer, bass.ds(c * CB, CB)],
                    direct[p0:128, layer, :].rearrange("p (b d) -> p b d", d=D),
                    AX.X, ALU.add).then_inc(s_summed[layer], 1)

            def step(layer, c, par):
                first = first_group(layer, c)
                for gi in range(GROUPS[layer]):
                    n = first + gi
                    if not isinstance(n, int) or n >= RING:
                        dve.wait_ge(s_zused, n - (RING - 1))
                    if gi == 0:
                        if layer == 0:
                            dve.wait_ge(s_rot[par], rot_count(c, par))
                        else:
                            dve.wait_ge(s_hready[layer], c + 1)
                            if layer == 1:
                                dve.wait_ge(s_xlo[par], x_count(c, par))
                    if gi == T1_LO // GT and layer == 1:
                        dve.wait_ge(s_xhi[par], x_count(c, par))
                    slot = group_slot(layer, par, gi) if not isinstance(n, int) else n % RING
                    last = min(GT, TILES[layer] - gi * GT)
                    for k in range(last):
                        t = gi * GT + k
                        p = (P0 if layer == 0 else 128) if t < TILES[layer] - 1 else KLAST[layer]
                        if layer == 0:
                            a, b = rot[0:p, par, t, :], base[0:p, par, :]
                        else:
                            a, b = xrep[0:p, par, t, :], h[0:p, layer - 1, :]
                        ins = nc.vector.tensor_tensor(z[0:p, slot, k, :], a, b, ALU.mult)
                    ins.then_inc(s_zready, 1)
                    if layer == 2 and gi == 1:
                        sum_over_d(1, c, c + 1)
                    if layer == 1 and gi == 1:
                        sum_over_d(0, c, c + 1)
                    if layer == 1 and gi == GROUPS[1] - 1 and not (isinstance(c, int) and c == 0):
                        sum_over_d(2, c - 1, c)

            def x_count(c, par):
                return (c - par) * 16 + 32

            def rot_count(c, par):
                return (c - par) * (8 * 6) + 16 * 6

            run_steps(dve, step)
            sum_over_d(2, CH - 1, CH)
            dve.wait_ge(s_y, 1)
            nc.vector.tensor_copy(y_sb[:, :], acc[2][0:1, :]).then_inc(s_yc, 1)

        @block.tensor
        def _(pe):
            pe.wait_ge(s_w0fold, 2)

            def step(layer, c, par):
                first = first_group(layer, c)
                if isinstance(c, int) and c == 0 and layer > 0:
                    pe.wait_ge(s_w[layer], 32)
                if not (isinstance(c, int) and c == 0):
                    pe.wait_ge(s_evac[layer], c)
                for gi in range(GROUPS[layer]):
                    n = first + gi
                    pe.wait_ge(s_zready, n + 1)
                    if layer == 2 and gi == 0 and par == 0 and not isinstance(c, int):
                        pe.wait_ge(s_w[2], 32)
                    slot = group_slot(layer, par, gi) if not isinstance(n, int) else n % RING
                    for k in range(min(GT, TILES[layer] - gi * GT)):
                        t = gi * GT + k
                        p = (P0 if layer == 0 else 128) if t < TILES[layer] - 1 else KLAST[layer]
                        mm = nc.tensor.matmul(acc[layer][:, :], w_sb[layer][0:p, t, :], z[0:p, slot, k, :],
                                              start=(t == 0), stop=(t == TILES[layer] - 1))
                    mm.then_inc(s_zused, 1)

            run_steps(pe, step)

            pe.wait_ge(s_wt, 16 * 6)
            pe.wait_ge(s_cols, 16)
            pe.wait_ge(s_summed[0], CH)
            pe.wait_ge(s_summed[1], CH)
            for m in range(H1 // 128):
                ms = slice(m * 128, (m + 1) * 128)
                nc.tensor.matmul(pm[m][:, :], wt1_sb[0:DC, 3, ms], zt[0:DC, 3, :], start=True, stop=False)
                for k in range(2):
                    nc.tensor.matmul(pm[m][:, :], wt1_sb[G:128, k, ms], zt[G:128, k, :], start=False, stop=False)
            pe.wait_ge(s_summed[2], CH)
            for m in range(H1 // 128):
                nc.tensor.matmul(pm[m][:, :], wt1_sb[:, 2, m * 128:(m + 1) * 128], zt[:, 2, :],
                                 start=False, stop=True).then_inc(s_m1, 1)
            for k in range(H1 // 128):
                pe.wait_ge(s_m1r, k + 1)
                for m in range(H2 // 128):
                    mm = nc.tensor.matmul(acc[m][:, :], wt2_sb[:, k, m * 128:(m + 1) * 128], m1[:, k, :],
                                          start=(k == 0), stop=(k == H1 // 128 - 1))
                    if k == H1 // 128 - 1:
                        mm.then_inc(s_m2, 1)
            pe.wait_ge(s_evac[2], CH)
            for k in range(H2 // 128):
                pe.wait_ge(s_m2r, k + 1)
                mm = nc.tensor.matmul(acc[2][0:1, :], wt3_sb[:, k:k + 1], m2[:, k, :],
                                      start=(k == 0), stop=(k == H2 // 128 - 1))
            mm.then_inc(s_y, 1)

        @block.scalar
        def _(act):
            act.wait_ge(s_cols, 16)

            def step(layer, c, par):
                first = first_group(layer, c)
                act.wait_ge(s_zused, first + GROUPS[layer])
                if layer < 2:
                    nc.scalar.activation(h[0:G, layer, :], acc[layer][0:G, :], ACT.Relu,
                                         bias=bias[0:G, layer:layer + 1])
                    nc.scalar.activation(h[G:128, layer, :], acc[layer][0:G, :], ACT.Relu,
                                         bias=bias[0:G, layer:layer + 1]).then_inc(s_hready[layer + 1], 1)
                if not (isinstance(c, int) and c == 0):
                    act.wait_ge(s_summed[layer], c)
                p0 = 0 if layer == 2 else G
                nc.scalar.activation(direct[p0:128, layer, :], acc[layer][p0:128, :], ACT.Relu,
                                     bias=bias[p0:128, layer:layer + 1]).then_inc(s_evac[layer], 1)

            run_steps(act, step)
            for m in range(H1 // 128):
                act.wait_ge(s_m1, m + 1)
                nc.scalar.activation(m1[:, m, :], pm[m][:, :], ACT.Relu, bias=bt1_sb[:, m:m + 1]).then_inc(s_m1r, 1)
            for m in range(H2 // 128):
                act.wait_ge(s_m2, m + 1)
                nc.scalar.activation(m2[:, m, :], acc[m][:, :], ACT.Relu, bias=bt2_sb[:, m:m + 1]).then_inc(s_m2r, 1)


def kernel(**inputs):
    import concourse.bacc as bacc
    from concourse.bass_utils import run_bass_kernel_spmd

    tables = [np.asarray(inputs[f"tbl_{f}"]) for f in range(F)]
    starts = np.cumsum([0] + [t.shape[0] for t in tables[:-1]]).astype(np.int32)
    ids = np.zeros((NG * FG, B), np.int32)
    ids[0:F] = np.asarray(inputs["ids"]).T
    offs = np.zeros((NG * FG, B), np.int32)
    offs[0:F] = starts[:, None]

    def spread(a):
        return np.ascontiguousarray(a.reshape(NG, FG, CH, CB).transpose(1, 3, 2, 0).reshape(128, CH * NG))

    g = np.arange(F)
    w0 = np.asarray(inputs["L0_rec_W0"]).reshape(F, F, S)
    w0a = np.concatenate([w0[g, (g + r) % F] for r in range(R)])
    w0b = np.concatenate([w0[(g + r) % F, g] for r in range(1, R)])
    arrays = {
        "tables": np.concatenate(tables), "ids": spread(ids), "offs": spread(offs)[:, 0:NG].copy(),
        "dense": np.ascontiguousarray(np.asarray(inputs["dense_ctx"]).T),
        "w0a": w0a, "w0b": w0b,
        "w1": np.asarray(inputs["L0_rec_W1"]), "w2": np.asarray(inputs["L0_rec_W2"]),
        "wt1": np.asarray(inputs["W_top1"]), "wt2": np.asarray(inputs["W_top2"]),
        "cols": np.ascontiguousarray(np.concatenate(
            [np.asarray(inputs[n]).reshape(-1, 128) for n in
             ("L0_rec_b0", "L0_rec_b1", "L0_rec_b2", "b_top1", "b_top2", "W_top3")]).T),
    }
    nc = bacc.Bacc("TRN2", target_bir_lowering=False, num_devices=1)
    args = [nc.dram_tensor(n, a.shape, mybir.dt.from_np(a.dtype), kind="ExternalInput").ap() for n, a in arrays.items()]
    out = nc.dram_tensor("out", (B, 1), F32, kind="ExternalOutput").ap()
    build(nc, *args, out)
    return run_bass_kernel_spmd(nc, [arrays], core_ids=[0]).results[0]["out"]
```

```python
from contextlib import ExitStack

import numpy as np
import concourse.bass as bass
from concourse import mybir

F32 = mybir.dt.float32
F32R = mybir.dt.float32r
I32 = mybir.dt.int32
ALU = mybir.AluOpType
ACT = mybir.ActivationFunctionType
AX = mybir.AxisListType

B, F, D = 512, 39, 16
S = 128
G = S // 2
CB = 32
N = CB * D
CH = B // CB
FG = 128 // CB
NG = -(-F // FG)
LAST = (F - (NG - 1) * FG) * CB
WRAP_G = 5
XROWS = F + WRAP_G * FG
R = F // 2 + 1
P0 = 3 * F
T0 = -(-R // 3)
K0_LAST = (R - 3 * (T0 - 1)) * F
T1 = -(-F // 2)
K1_LAST = (F - 2 * (T1 - 1)) * G
TH = T1 // 2
H1, H2 = 512, 256
ZD = 2 * S
DC = 16

TILES = [T0, T1, T1]
KLAST = [K0_LAST, K1_LAST, K1_LAST]

PLAN = [
    [("S", 0, 3), ("N", 3, 4)],
    [("S", 0, 3), ("N", 3, 4), ("S", 7, 3), ("N", 10, 4), ("S", 14, 3), ("N", 17, 3)],
    [("N", 19, 1), ("N", 17, 2), ("S", 10, 3), ("N", 13, 4), ("S", 0, 3), ("N", 3, 4), ("N", 7, 3)],
]
PE_ORDER = [[1, 0], [1, 0, 3, 2, 5, 4], [0, 1, 3, 2, 5, 6, 4]]
HALF_DONE = [None, 3, 4]
NMAX, SMAX = 4, 3
RING = {"N": 3, "S": 3}
PER_LAYER = {k: [sum(g[0] == k for g in p) for p in PLAN] for k in "NS"}
PER_CHUNK = {k: sum(v) for k, v in PER_LAYER.items()}
S_TILES = SMAX * PER_CHUNK["S"]
assert all(PER_CHUNK[k] % RING[k] == 0 for k in "NS") and CH % 2 == 0
assert all(sorted(t for _, a, n in p for t in range(a, a + n)) == list(range(TILES[l])) for l, p in enumerate(PLAN))


W_LOADS = sum(1 + (t + n == T1 and n > 1) for p in PLAN[1:] for _, t, n in p)


def first_group(kind, layer, c):
    n0, n1, n2 = PER_LAYER[kind]
    each = PER_CHUNK[kind]
    if layer == 1:
        return c * each + n0
    if layer == 2:
        return CH * each - n2 if isinstance(c, int) and c == CH - 1 else c * each + 2 * n0 + n1
    return 0 if isinstance(c, int) and c == 0 else c * each - n2


def group_number(layer, c, i):
    kind = PLAN[layer][i][0]
    at = sum(g[0] == kind for g in PLAN[layer][:i])
    number = first_group(kind, layer, c) + at
    slot = (number if isinstance(number, int) else first_group(kind, layer, 2) + at) % RING[kind]
    return number, slot


def s_weight(layer, i):
    return SMAX * (sum(PER_LAYER["S"][:layer]) + sum(g[0] == "S" for g in PLAN[layer][:i]))


def n_weight(layer, i):
    return sum(g[2] for g in PLAN[layer][:i] if g[0] == "N")


def run_steps(eng, step):
    step(0, 0, 0)
    step(1, 0, 0)
    step(0, 1, 1)
    with eng.Fori(0, CH - 2, 2) as c0:
        for u in range(2):
            step(2, c0 + u, u)
            step(1, c0 + (u + 1), (u + 1) % 2)
            step(0, c0 + (u + 2), u)
    step(2, CH - 2, 0)
    step(1, CH - 1, 1)
    step(2, CH - 1, 1)


def is_chunk(c, k):
    return isinstance(c, int) and c == k


def build(nc, tables, ids, offs, dense, w0a, w0b, w1, w2, wt1, wt2, cols, out):
    with ExitStack() as ctx:
        def sb(name, shape, dt=F32):
            return ctx.enter_context(nc.sbuf_tensor(name, shape, dt))

        def psum(name, shape):
            return ctx.enter_context(nc.psum_tensor(name, shape, F32))

        def sem(name):
            return ctx.enter_context(nc.semaphore(name))

        xt = nc.dram_tensor("xt_scratch", (CH, XROWS, N), F32, kind="Internal").ap()

        ids_sb = sb("ids_sb", [128, CH * NG], I32)
        offs_sb = sb("offs_sb", [128, NG], I32)
        idx_sb = sb("idx_sb", [128, 2, NG], I32)
        gath = sb("gath", [128, 2, NG, D])
        wn_sb = [sb(f"wn{l}", [128, sum(g[2] for g in PLAN[l] if g[0] == "N"), S]) for l in range(3)]
        wh_sb = sb("wh_sb", [128, S_TILES, S], F32R)
        wl_sb = sb("wl_sb", [128, S_TILES, S], F32R)
        cols_sb = sb("cols_sb", [128, 3 + H1 // 128 + 2 * (H2 // 128)])
        bias = cols_sb[:, 0:3]
        bt1_sb = cols_sb[:, 3:3 + H1 // 128]
        bt2_sb = cols_sb[:, 3 + H1 // 128:3 + (H1 + H2) // 128]
        wt3_sb = cols_sb[:, 3 + (H1 + H2) // 128:3 + (H1 + 2 * H2) // 128]
        base = sb("base", [128, N])
        rot = sb("rot", [128, T0, N])
        xlo = sb("xlo", [128, 2, TH, N])
        xhi = sb("xhi", [128, T1 - TH, N])
        zn = sb("zn", [128, RING["N"], NMAX, N])
        zs = sb("zs", [128, RING["S"], SMAX, N])
        zh = sb("zh", [128, RING["S"], SMAX, N], F32R)
        zl = sb("zl", [128, RING["S"], SMAX, N], F32R)
        direct = sb("direct", [128, 3, N])
        zt = sb("zt", [128, 4, B])
        y_sb = sb("y_sb", [1, B])
        w0a_sb = zn[:, 0, :, :].rearrange("p a (b s) -> p (a b) s", s=S)
        w0b_sb = zn[:, 1, :, :].rearrange("p a (b s) -> p (a b) s", s=S)
        wst = zs[:, 0:2, :, :].rearrange("p r a (b s) -> p (r a b) s", s=S)
        m1 = zn[:, 0, 0:H1 // 128, :]
        m2 = zn[:, 1, 0:H2 // 128, :]
        wt1_sb = rot[:, 0:4, :]
        wt2_sb = rot[:, 4:6, :].rearrange("p a (b n) -> p (a b) n", n=H2)

        acc = [psum(f"acc{i}", [128, N]) for i in range(3)]
        h_ps = [psum(f"h{i}", [128, N]) for i in range(2)]
        base_ps = psum("base_ps", [128, N])
        pm = [psum(f"pm{i}", [128, B]) for i in range(2)] + h_ps

        s_ids = sem("s_ids")
        s_idx = sem("s_idx")
        s_w0 = sem("s_w0")
        s_w0zero = sem("s_w0zero")
        s_fold = sem("s_fold")
        s_w = sem("s_w")
        s_wh = sem("s_wh")
        s_wl = sem("s_wl")
        s_cols = sem("s_cols")
        s_wt = sem("s_wt")
        s_gathered = [sem(f"s_gathered{i}") for i in range(2)]
        s_stored = [sem(f"s_stored{i}") for i in range(2)]
        s_rot = sem("s_rot")
        s_base = sem("s_base")
        s_xlo = [sem(f"s_xlo{i}") for i in range(2)]
        s_xhi = sem("s_xhi")
        s_ready = {"N": sem("s_nready"), "S": sem("s_sready")}
        s_used = {"N": sem("s_nused"), "S": sem("s_sused")}
        s_hi = sem("s_hi")
        s_lo = sem("s_lo")
        s_hready = [None, sem("s_hready1"), sem("s_hready2")]
        s_evac = [sem(f"s_evac{i}") for i in range(3)]
        s_summed = [sem(f"s_summed{i}") for i in range(3)]
        s_m1 = sem("s_m1")
        s_m1r = sem("s_m1r")
        s_m2 = sem("s_m2")
        s_m2r = sem("s_m2r")
        s_y = sem("s_y")
        s_yc = sem("s_yc")
        s_out = sem("s_out")

        def done(eng, layer, c, groups):
            kind = PLAN[layer][groups - 1][0]
            k = sum(g[0] == kind for g in PLAN[layer][:groups])
            eng.wait_ge(s_ready[kind], first_group(kind, layer, c) + k)

        block = ctx.enter_context(nc.Block())

        @block.gpsimd
        def _(pool):
            nc.gpsimd.memset(w0b_sb[0:64, 0, :], 0.0).then_inc(s_w0zero, 1)
            pool.wait_ge(s_ids, 32)

            def index(c, slot):
                nc.gpsimd.tensor_tensor(idx_sb[:, slot, :], ids_sb[:, bass.ds(c * NG, NG)], offs_sb[:, :],
                                        ALU.add).then_inc(s_idx, 1)

            def gather(slot, js):
                for j in js:
                    p = 128 if j < NG - 1 else LAST
                    nc.gpsimd.indirect_dma_start(
                        gath[0:p, slot, j, :], None, tables,
                        bass.IndirectOffsetOnAxis(ap=idx_sb[0:p, slot, j:j + 1], axis=0),
                    ).then_inc(s_gathered[slot], 16)

            def indexed(c):
                pool.wait_ge(s_idx, c + 1)
                pool.nop(nofuse=True)

            def low(layer, c, i):
                number, slot = group_number(layer, c, i)
                tiles = PLAN[layer][i][2]
                p = P0 if layer == 0 else 128
                pool.wait_ge(s_hi, number + 1)
                nc.gpsimd.tensor_tensor(zl[0:p, slot, 0:tiles, :], zs[0:p, slot, 0:tiles, :],
                                        zh[0:p, slot, 0:tiles, :].bitcast(F32), ALU.subtract).then_inc(s_lo, 1)

            def lows(layer, c):
                for i, g in enumerate(PLAN[layer]):
                    if g[0] == "S":
                        low(layer, c, i)

            def body(c, slot, stored):
                work = [(l, d, i) for l, d in ((2, 0), (1, 1), (0, 2)) for i, g in enumerate(PLAN[l]) if g[0] == "S"]
                per = -(-NG // (len(work) - 1))
                for k, (l, d, i) in enumerate(work):
                    low(l, c + d, i)
                    if stored is not None:
                        if k == 0:
                            pool.wait_ge(s_stored[slot], stored)
                            index(c + 3, slot)
                            indexed(c + 3)
                        gather(slot, range(k * per, min(NG, k * per + per)))

            for c in range(2):
                index(c, c)
                indexed(c)
                gather(c, range(NG))
            pool.wait_ge(s_stored[0], 48)
            index(2, 0)
            indexed(2)
            gather(0, range(NG))
            lows(0, 0)
            lows(1, 0)
            lows(0, 1)
            with pool.Fori(0, (CH - 4) // 2) as i:
                for u in range(2):
                    body(i * 2 + u, 1 - u, i * 48 + 48 * (u + 1))
            body(CH - 4, 1, 48 * ((CH - 4) // 2 + 1))
            body(CH - 3, 0, None)
            lows(2, CH - 2)
            lows(1, CH - 1)
            lows(2, CH - 1)

        @block.sync
        def _(sp):
            sp.dma_start(ids_sb[:, :], ids).then_inc(s_ids, 16)
            sp.dma_start(offs_sb[:, :], offs).then_inc(s_ids, 16)

            def store(c, slot, n):
                sp.wait_ge(s_gathered[slot], n * (16 * NG))
                g = gath[:, slot, :, :]
                m = (NG - 1) * FG
                sp.dma_start(xt[c, 0:m, :].rearrange("(j q) (b d) -> (q b) j d", q=FG, d=D),
                             g[:, 0:NG - 1, :]).then_inc(s_stored[slot], 16)
                sp.dma_start(xt[c, m:F, :].rearrange("q (b d) -> (q b) d", d=D),
                             g[0:LAST, NG - 1, :]).then_inc(s_stored[slot], 16)
                sp.dma_start(xt[c, F:XROWS, :].rearrange("(j q) (b d) -> (q b) j d", q=FG, d=D),
                             g[:, 0:WRAP_G, :]).then_inc(s_stored[slot], 16)

            def fields(c, first, dims):
                return bass.AP(tensor=xt.tensor, offset=c * (XROWS * N) + first * N,
                               ap=[[n * N, count] for n, count in dims] + [[1, N]])

            def load_rot(c):
                for j in range(3):
                    nt = (R - j + 2) // 3
                    sp.dma_start(base[j * F:(j + 1) * F, :], fields(c, 0, [[1, F]])).then_inc(s_rot, 16)
                    sp.dma_start(rot[j * F:(j + 1) * F, 0:nt, :],
                                 fields(c, j, [[1, F], [3, nt]])).then_inc(s_rot, 16)

            def load_x(c, dst, t0, t1, s):
                for half in range(2):
                    tn = t1 if half == 0 or t1 < T1 else F // 2
                    sp.dma_start(dst[half * G:(half + 1) * G, 0:tn - t0, :],
                                 fields(c, 2 * t0 + half, [[0, G], [2, tn - t0]])).then_inc(s, 16)

            def load_lo(c, slot):
                load_x(c, xlo[:, slot, :, :], 0, TH, s_xlo[slot])

            def load_hi(c):
                load_x(c, xhi[:, :, :], TH, T1, s_xhi)

            store(0, 0, 1)
            sp.wait_ge(s_stored[0], 48)
            load_rot(0)
            load_lo(0, 0)
            load_hi(0)
            store(1, 1, 1)
            sp.wait_ge(s_stored[1], 48)
            done(sp, 0, 0, len(PLAN[0]))
            load_rot(1)
            load_lo(1, 1)

            with sp.Fori(1, CH // 2) as i:
                for u in range(2):
                    c = i * 2 + u
                    store(c, u, i + 1)
                    sp.wait_ge(s_stored[u], i * 48 + 48)
                    done(sp, 0, c - 1, len(PLAN[0]))
                    load_rot(c)
                    done(sp, 2, c - 2, HALF_DONE[2])
                    load_hi(c - 1)
                    done(sp, 2, c - 2, len(PLAN[2]))
                    load_lo(c, u)
            done(sp, 2, CH - 2, HALF_DONE[2])
            load_hi(CH - 1)
            done(sp, 0, CH - 1, len(PLAN[0]))
            sp.dma_start(wt1_sb[G:128, 0, :], wt1[0:G, :]).then_inc(s_wt, 16)
            sp.dma_start(wt1_sb[G:128, 1, :], wt1[G:2 * G, :]).then_inc(s_wt, 16)
            sp.dma_start(wt1_sb[:, 2, :], wt1[2 * G:ZD, :]).then_inc(s_wt, 16)
            sp.dma_start(wt1_sb[0:DC, 3, :], wt1[ZD:ZD + DC, :]).then_inc(s_wt, 16)
            sp.dma_start(zt[0:DC, 3, :], dense).then_inc(s_wt, 16)
            sp.dma_start(wt2_sb, wt2.rearrange("(k p) n -> p k n", p=128)).then_inc(s_wt, 16)
            sp.wait_ge(s_yc, 1)
            sp.dma_start(out.rearrange("b o -> o b"), y_sb[:, :]).then_inc(s_out, 16)
            sp.wait_ge(s_out, 16)

        @block.vector
        def _(dve):
            dve.wait_ge(s_w0zero, 1)
            dve.wait_ge(s_w0, 80)
            for i, (kind, t0, n) in enumerate(PLAN[0]):
                dst, at = (wn_sb[0], n_weight(0, i)) if kind == "N" else (wst, s_weight(0, i))
                whole = n - (t0 + n == T0)
                nc.vector.tensor_tensor(dst[0:P0, at:at + whole, :], w0a_sb[0:P0, t0:t0 + whole, :],
                                        w0b_sb[0:P0, t0:t0 + whole, :], ALU.add).then_inc(s_fold, 1)
                if t0 + n == T0:
                    nc.vector.tensor_tensor(dst[0:K0_LAST, at + whole, :], w0a_sb[0:K0_LAST, T0 - 1, :],
                                            w0b_sb[0:K0_LAST, T0 - 1, :], ALU.add).then_inc(s_fold, 1)
            for l in range(3):
                a, b = SMAX * sum(PER_LAYER["S"][:l]), SMAX * sum(PER_LAYER["S"][:l + 1])
                p = P0 if l == 0 else 128
                dve.wait_ge(s_wh, l + 1)
                nc.vector.tensor_tensor(wl_sb[0:p, a:b, :], wst[0:p, a:b, :], wh_sb[0:p, a:b, :].bitcast(F32),
                                        ALU.subtract).then_inc(s_wl, 1)
            dve.wait_ge(s_wl, 3)

            def sum_over_d(layer, c, n):
                p0 = 0 if layer == 2 else G
                dve.wait_ge(s_evac[layer], n)
                nc.vector.tensor_reduce(
                    zt[p0:128, layer, bass.ds(c * CB, CB)],
                    direct[p0:128, layer, :].rearrange("p (b d) -> p b d", d=D),
                    AX.X, ALU.add).then_inc(s_summed[layer], 1)

            def x_tiles(layer, par, p, t, n):
                if layer == 0:
                    return rot[0:p, t:t + n, :]
                return xlo[0:p, par, t:t + n, :] if t < TH else xhi[0:p, t - TH:t - TH + n, :]

            def step(layer, c, par):
                for i, (kind, t0, n) in enumerate(PLAN[layer]):
                    number, slot = group_number(layer, c, i)
                    if not isinstance(number, int) or number >= RING[kind]:
                        dve.wait_ge(s_used["N"] if kind == "N" else s_lo, number - (RING[kind] - 1))
                    if i == 0 and layer == 0:
                        dve.wait_ge(s_rot, c * 96 + 96)
                        dve.wait_ge(s_base, c + 1)
                    if i == 0 and layer > 0:
                        dve.wait_ge(s_hready[layer], c + 1)
                    if i == 0 and layer == 1:
                        dve.wait_ge(s_xlo[par], (c - par) * 16 + 32)
                    if i == HALF_DONE[1] and layer == 1:
                        dve.wait_ge(s_xhi, c * 32 + 32)
                    other = base_ps if layer == 0 else h_ps[layer - 1]
                    p = P0 if layer == 0 else 128
                    z = zn if kind == "N" else zs
                    ragged = t0 + n == TILES[layer]
                    if n > ragged:
                        m = n - ragged
                        ins = nc.vector.tensor_tensor(z[0:p, slot, 0:m, :], x_tiles(layer, par, p, t0, m),
                                                      other[0:p, :].unsqueeze(1).broadcast_to([p, m, N]), ALU.mult)
                    if ragged:
                        k = KLAST[layer]
                        ins = nc.vector.tensor_tensor(z[0:k, slot, n - 1, :], x_tiles(layer, par, k, t0 + n - 1, 1)[:, 0, :],
                                                      other[0:k, :], ALU.mult)
                    ins.then_inc(s_ready[kind], 1)
                    if layer == 2 and i == 2:
                        sum_over_d(1, c, c + 1)
                    if layer == 1 and i == 2:
                        sum_over_d(0, c, c + 1)
                if layer == 0 and not isinstance(c, int):
                    sum_over_d(2, c - 2, c - 1)
                if layer == 2 and is_chunk(c, CH - 1):
                    sum_over_d(2, c - 1, c)

            run_steps(dve, step)
            sum_over_d(2, CH - 1, CH)
            dve.wait_ge(s_y, 1)
            nc.vector.tensor_copy(y_sb[:, :], acc[2][0:1, :]).then_inc(s_yc, 1)

        @block.tensor
        def _(pe):
            pe.wait_ge(s_fold, 1 + len(PLAN[0]))
            pe.wait_ge(s_wl, 3)

            def step(layer, c, par):
                if is_chunk(c, 0) and layer == 1:
                    pe.wait_ge(s_w, W_LOADS * 16)
                if layer < 2 and not is_chunk(c, 0):
                    pe.wait_ge(s_evac[layer], c)
                if layer == 0 and not isinstance(c, int):
                    pe.wait_ge(s_evac[2], c - 1)
                if layer == 2 and is_chunk(c, CH - 1):
                    pe.wait_ge(s_evac[2], c)
                out_ps = acc[layer][:, :]
                for o, i in enumerate(PE_ORDER[layer]):
                    kind, t0, n = PLAN[layer][i]
                    number, slot = group_number(layer, c, i)
                    pe.wait_ge(s_ready["N"] if kind == "N" else s_lo, number + 1)
                    for k in range(n):
                        t = t0 + k
                        p = (P0 if layer == 0 else 128) if t < TILES[layer] - 1 else KLAST[layer]
                        first, last = o == 0 and k == 0, o == len(PLAN[layer]) - 1 and k == n - 1
                        if kind == "N":
                            mm = nc.tensor.matmul(out_ps, wn_sb[layer][0:p, n_weight(layer, i) + k, :],
                                                  zn[0:p, slot, k, :], start=first, stop=last)
                        else:
                            a = s_weight(layer, i) + k
                            nc.tensor.matmul(out_ps, wl_sb[0:p, a, :], zh[0:p, slot, k, :], start=first, stop=False)
                            nc.tensor.matmul(out_ps, wh_sb[0:p, a, :], zl[0:p, slot, k, :], start=False, stop=False)
                            mm = nc.tensor.matmul(out_ps, wh_sb[0:p, a, :], zh[0:p, slot, k, :], start=False, stop=last)
                    mm.then_inc(s_used[kind], 1)

            run_steps(pe, step)

            pe.wait_ge(s_wt, 16 * 6)
            pe.wait_ge(s_cols, 16)
            pe.wait_ge(s_summed[0], CH)
            pe.wait_ge(s_summed[1], CH)
            for m in range(H1 // 128):
                ms = slice(m * 128, (m + 1) * 128)
                nc.tensor.matmul(pm[m][:, :], wt1_sb[0:DC, 3, ms], zt[0:DC, 3, :], start=True, stop=False)
                for k in range(2):
                    nc.tensor.matmul(pm[m][:, :], wt1_sb[G:128, k, ms], zt[G:128, k, :], start=False, stop=False)
            pe.wait_ge(s_summed[2], CH)
            for m in range(H1 // 128):
                nc.tensor.matmul(pm[m][:, :], wt1_sb[:, 2, m * 128:(m + 1) * 128], zt[:, 2, :],
                                 start=False, stop=True).then_inc(s_m1, 1)
            for k in range(H1 // 128):
                pe.wait_ge(s_m1r, k + 1)
                for m in range(H2 // 128):
                    mm = nc.tensor.matmul(acc[m][:, :], wt2_sb[:, k, m * 128:(m + 1) * 128], m1[:, k, :],
                                          start=(k == 0), stop=(k == H1 // 128 - 1))
                    if k == H1 // 128 - 1:
                        mm.then_inc(s_m2, 1)
            pe.wait_ge(s_evac[2], CH)
            for k in range(H2 // 128):
                pe.wait_ge(s_m2r, k + 1)
                mm = nc.tensor.matmul(acc[2][0:1, :], wt3_sb[:, k:k + 1], m2[:, k, :],
                                      start=(k == 0), stop=(k == H2 // 128 - 1))
            mm.then_inc(s_y, 1)

        @block.scalar
        def _(act):
            act.dma_start(w0a_sb[0:P0, 0:T0 - 1, :], w0a[0:P0 * (T0 - 1), :].rearrange("(t p) s -> p t s", p=P0)
                          ).then_inc(s_w0, 16)
            act.dma_start(w0a_sb[0:K0_LAST, T0 - 1, :], w0a[P0 * (T0 - 1):, :]).then_inc(s_w0, 16)
            act.wait_ge(s_w0zero, 1)
            act.dma_start(w0b_sb[F:P0, 0, :], w0b[0:2 * F, :]).then_inc(s_w0, 16)
            act.dma_start(w0b_sb[0:P0, 1:T0 - 1, :],
                          w0b[2 * F:2 * F + P0 * (T0 - 2), :].rearrange("(t p) s -> p t s", p=P0)
                          ).then_inc(s_w0, 16)
            act.dma_start(w0b_sb[0:K0_LAST, T0 - 1, :], w0b[2 * F + P0 * (T0 - 2):, :]).then_inc(s_w0, 16)
            for l, w in ((1, w1), (2, w2)):
                for i, (kind, t0, n) in enumerate(PLAN[l]):
                    dst, at = (wn_sb[l], n_weight(l, i)) if kind == "N" else (wst, s_weight(l, i))
                    whole = n - (t0 + n == T1)
                    if whole:
                        act.dma_start(dst[:, at:at + whole, :],
                                      w[t0 * 128:(t0 + whole) * 128, :].rearrange("(t p) s -> p t s", p=128)
                                      ).then_inc(s_w, 16)
                    if whole < n:
                        act.dma_start(dst[0:K1_LAST, at + whole, :], w[(T1 - 1) * 128:, :]).then_inc(s_w, 16)
            act.dma_start(cols_sb[:, :], cols).then_inc(s_cols, 16)
            for l in range(3):
                a, b = SMAX * sum(PER_LAYER["S"][:l]), SMAX * sum(PER_LAYER["S"][:l + 1])
                p = P0 if l == 0 else 128
                if l == 0:
                    act.wait_ge(s_fold, 1)
                else:
                    act.wait_ge(s_w, W_LOADS * 16)
                nc.scalar.copy(wh_sb[0:p, a:b, :], wst[0:p, a:b, :]).then_inc(s_wh, 1)
            act.wait_ge(s_cols, 16)

            def high(layer, c, groups):
                p = P0 if layer == 0 else 128
                for i in groups:
                    if PLAN[layer][i][0] == "S":
                        number, slot = group_number(layer, c, i)
                        n = PLAN[layer][i][2]
                        act.wait_ge(s_ready["S"], number + 1)
                        if not isinstance(number, int) or number >= RING["S"]:
                            act.wait_ge(s_used["S"], number - (RING["S"] - 1))
                        nc.scalar.copy(zh[0:p, slot, 0:n, :], zs[0:p, slot, 0:n, :]).then_inc(s_hi, 1)

            def copy_base(c):
                act.wait_ge(s_rot, c * 96 + 96)
                if not is_chunk(c, 0):
                    done(act, 0, c - 1, len(PLAN[0]))
                nc.scalar.copy(base_ps[0:P0, :], base[0:P0, :]).then_inc(s_base, 1)

            def finish(layer, c):
                for kind in "NS":
                    act.wait_ge(s_used[kind], first_group(kind, layer, c) + PER_LAYER[kind][layer])
                if layer < 2:
                    nc.scalar.activation(h_ps[layer][0:G, :], acc[layer][0:G, :], ACT.Relu,
                                         bias=bias[0:G, layer:layer + 1])
                    nc.scalar.activation(h_ps[layer][G:128, :], acc[layer][0:G, :], ACT.Relu,
                                         bias=bias[0:G, layer:layer + 1]).then_inc(s_hready[layer + 1], 1)
                    if not is_chunk(c, 0):
                        act.wait_ge(s_summed[layer], c)
                elif is_chunk(c, CH - 1):
                    act.wait_ge(s_summed[2], c)
                p0 = 0 if layer == 2 else G
                nc.scalar.activation(direct[p0:128, layer, :], acc[layer][p0:128, :], ACT.Relu,
                                     bias=bias[p0:128, layer:layer + 1]).then_inc(s_evac[layer], 1)

            def step(layer, c, par):
                s_at = [i for i, g in enumerate(PLAN[layer]) if g[0] == "S"]
                if layer == 0:
                    if isinstance(c, int):
                        copy_base(c)
                    high(0, c, s_at)
                    if not is_chunk(c, 0):
                        finish(1, c - 1)
                        if not isinstance(c, int):
                            act.wait_ge(s_summed[2], c - 1)
                elif layer == 1:
                    if is_chunk(c, 0):
                        finish(0, c)
                        high(1, c, s_at)
                    else:
                        high(1, c, s_at[:1])
                        finish(2, c - 1)
                        if not is_chunk(c, CH - 1):
                            copy_base(c + 1)
                        high(1, c, s_at[1:])
                else:
                    if is_chunk(c, CH - 1):
                        finish(1, c)
                        high(2, c, s_at)
                        finish(2, c)
                    else:
                        high(2, c, s_at[:1])
                        finish(0, c + 1)
                        high(2, c, s_at[1:])

            run_steps(act, step)
            for m in range(H1 // 128):
                act.wait_ge(s_m1, m + 1)
                nc.scalar.activation(m1[:, m, :], pm[m][:, :], ACT.Relu, bias=bt1_sb[:, m:m + 1]).then_inc(s_m1r, 1)
            for m in range(H2 // 128):
                act.wait_ge(s_m2, m + 1)
                nc.scalar.activation(m2[:, m, :], acc[m][:, :], ACT.Relu, bias=bt2_sb[:, m:m + 1]).then_inc(s_m2r, 1)


def kernel(**inputs):
    import concourse.bacc as bacc
    from concourse.bass_utils import run_bass_kernel_spmd

    tables = [np.asarray(inputs[f"tbl_{f}"]) for f in range(F)]
    starts = np.cumsum([0] + [t.shape[0] for t in tables[:-1]]).astype(np.int32)
    ids = np.zeros((NG * FG, B), np.int32)
    ids[0:F] = np.asarray(inputs["ids"]).T
    offs = np.zeros((NG * FG, B), np.int32)
    offs[0:F] = starts[:, None]

    def spread(a):
        return np.ascontiguousarray(a.reshape(NG, FG, CH, CB).transpose(1, 3, 2, 0).reshape(128, CH * NG))

    g = np.arange(F)
    w0 = np.asarray(inputs["L0_rec_W0"]).reshape(F, F, S)
    w0a = np.concatenate([w0[g, (g + r) % F] for r in range(R)])
    w0b = np.concatenate([w0[(g + r) % F, g] for r in range(1, R)])
    arrays = {
        "tables": np.concatenate(tables), "ids": spread(ids), "offs": spread(offs)[:, 0:NG].copy(),
        "dense": np.ascontiguousarray(np.asarray(inputs["dense_ctx"]).T),
        "w0a": w0a, "w0b": w0b,
        "w1": np.asarray(inputs["L0_rec_W1"]), "w2": np.asarray(inputs["L0_rec_W2"]),
        "wt1": np.asarray(inputs["W_top1"]), "wt2": np.asarray(inputs["W_top2"]),
        "cols": np.ascontiguousarray(np.concatenate(
            [np.asarray(inputs[n]).reshape(-1, 128) for n in
             ("L0_rec_b0", "L0_rec_b1", "L0_rec_b2", "b_top1", "b_top2", "W_top3")]).T),
    }
    nc = bacc.Bacc("TRN2", target_bir_lowering=False, num_devices=1)
    args = [nc.dram_tensor(n, a.shape, mybir.dt.from_np(a.dtype), kind="ExternalInput").ap() for n, a in arrays.items()]
    out = nc.dram_tensor("out", (B, 1), F32, kind="ExternalOutput").ap()
    build(nc, *args, out)
    return run_bass_kernel_spmd(nc, [arrays], core_ids=[0]).results[0]["out"]
```

```python
from contextlib import ExitStack

import numpy as np
import concourse.bass as bass
from concourse import mybir

F32 = mybir.dt.float32
F32R = mybir.dt.float32r
I32 = mybir.dt.int32
ALU = mybir.AluOpType
ACT = mybir.ActivationFunctionType
AX = mybir.AxisListType

B, F, D = 512, 39, 16
S = 128
G = S // 2
CB = 32
N = CB * D
CH = B // CB
FG = 128 // CB
NG = -(-F // FG)
LAST = (F - (NG - 1) * FG) * CB
WRAP_G = 5
XROWS = F + WRAP_G * FG
R = F // 2 + 1
P0 = 3 * F
T0 = -(-R // 3)
K0_LAST = (R - 3 * (T0 - 1)) * F
T1 = -(-F // 2)
K1_LAST = (F - 2 * (T1 - 1)) * G
TH = T1 // 2
H1, H2 = 512, 256
ZD = 2 * S
DC = 16
ROT_FIRST = 3
EARLY_M, EARLY = 2, B - CB
WARM0, WARM1 = 14000, 12000
BEFORE_L0 = 3
SCRATCH = 8192

TILES = [T0, T1, T1]
KLAST = [K0_LAST, K1_LAST, K1_LAST]

PLAN = [
    [("S", 0, 3), ("N", 3, 4)],
    [("S", 0, 3), ("N", 3, 3), ("D", 6, 2), ("S", 8, 2), ("D", 19, 1), ("S", 10, 2), ("N", 12, 3),
     ("D", 15, 2), ("S", 17, 2)],
    [("S", 10, 1), ("N", 11, 2), ("S", 13, 3), ("N", 16, 3), ("D", 19, 1), ("S", 0, 2), ("N", 2, 4),
     ("D", 6, 2), ("S", 8, 2)],
]
PE_ORDER = [[1, 0], [1, 2, 0, 3, 4, 6, 5, 7, 8], [0, 1, 3, 2, 4, 6, 7, 5, 8]]
HALF_DONE = [None, 4, 5]
RING = {"N": 2, "S": 3, "D": 2}
ZS_RING = 2
FINISH_AT = [9, 3, 2]
GATHERS = [2, 0, 3, 1, 0, 2, 1, 1, 0]
MOST = {k: max(n for p in PLAN for kind, _, n in p if kind == k) for k in "NSD"}
PER_LAYER = {k: [sum(g[0] == k for g in p) for p in PLAN] for k in "NSD"}
PER_CHUNK = {k: sum(v) for k, v in PER_LAYER.items()}
SPLIT_AT = [sum(n for p in PLAN[:l] for kind, _, n in p if kind != "N") for l in range(4)]
assert all(2 * PER_CHUNK[k] % RING[k] == 0 for k in "NSD") and 2 * PER_CHUNK["S"] % ZS_RING == 0 and CH % 2 == 0
assert N == B
assert K1_LAST == G and 2 * G == 128
assert sum(GATHERS) == NG and len(GATHERS) == PER_CHUNK["S"]
for l, p in enumerate(PLAN):
    assert sorted(t for _, a, n in p for t in range(a, a + n)) == list(range(TILES[l]))
    assert all(kind == "N" or (kind == "D" and n == 1 and l > 0) for kind, t, n in p if t + n == TILES[l])


W_LOADS = [sum(1 + (t + n == TILES[l] and (n > 1 or kind != "N")) for kind, t, n in p)
           for l, p in enumerate(PLAN)]


def folded(layer, i):
    kind, t, n = PLAN[layer][i]
    return kind != "N" and t + n == TILES[layer]


def group_rows(layer, i):
    return KLAST[layer] if folded(layer, i) else P0 if layer == 0 else 128


FOLDS = sum(1 + (t + n == T0 and n > 1) for _, t, n in PLAN[0])


def first_group(kind, layer, c):
    n0, n1, n2 = PER_LAYER[kind]
    each = PER_CHUNK[kind]
    if layer == 1:
        return c * each + n0
    if layer == 2:
        return CH * each - n2 if isinstance(c, int) and c == CH - 1 else c * each + 2 * n0 + n1
    return 0 if isinstance(c, int) and c == 0 else c * each - n2


def group_number(layer, c, par, i, ring=None):
    kind = PLAN[layer][i][0]
    at = sum(g[0] == kind for g in PLAN[layer][:i])
    number = first_group(kind, layer, c) + at
    like = number if isinstance(number, int) else first_group(kind, layer, par + 2) + at
    return number, like % (ring or RING[kind])


def s_weight(layer, i):
    return SPLIT_AT[layer] + sum(g[2] for g in PLAN[layer][:i] if g[0] != "N")


def n_weight(layer, i):
    return sum(g[2] for g in PLAN[layer][:i] if g[0] == "N")


def run_steps(eng, step):
    step(0, 0, 0)
    step(1, 0, 0)
    step(0, 1, 1)
    with eng.Fori(0, CH - 2, 2) as c0:
        for u in range(2):
            step(2, c0 + u, u)
            step(1, c0 + (u + 1), (u + 1) % 2)
            step(0, c0 + (u + 2), u)
    step(2, CH - 2, 0)
    step(1, CH - 1, 1)
    step(2, CH - 1, 1)


def is_chunk(c, k):
    return isinstance(c, int) and c == k


def build(nc, tables, ids, dense, w0a, w0b, w1, w2, wt1, wt2, cols, out):
    with ExitStack() as ctx:
        def sb(name, shape, dt=F32):
            return ctx.enter_context(nc.sbuf_tensor(name, shape, dt))

        def psum(name, shape):
            return ctx.enter_context(nc.psum_tensor(name, shape, F32))

        def sem(name):
            return ctx.enter_context(nc.semaphore(name))

        xt = nc.dram_tensor("xt_scratch", (CH, XROWS, N), F32, kind="Internal").ap()

        ids_sb = sb("ids_sb", [128, (CH + 1) * NG], I32)
        starts_sb = ids_sb[:, CH * NG:]
        idx_sb = sb("idx_sb", [128, 2, NG], I32)
        gath = sb("gath", [128, 2, NG, D])
        wn_sb = [sb(f"wn{l}", [128, sum(g[2] for g in PLAN[l] if g[0] == "N"), S]) for l in range(3)]
        wh_sb = sb("wh_sb", [128, SPLIT_AT[3], S], F32R)
        wl_sb = sb("wl_sb", [128, SPLIT_AT[3], S], F32R)
        cols_sb = sb("cols_sb", [128, 3 + H1 // 128 + 2 * (H2 // 128)])
        bias = cols_sb[:, 0:3]
        bt1_sb = cols_sb[:, 3:3 + H1 // 128]
        bt2_sb = cols_sb[:, 3 + H1 // 128:3 + (H1 + H2) // 128]
        wt3_sb = cols_sb[:, 3 + (H1 + H2) // 128:3 + (H1 + 2 * H2) // 128]
        base = sb("base", [128, N])
        rot = sb("rot", [128, T0, N])
        xlo = sb("xlo", [128, 2, TH, N])
        xhi = sb("xhi", [128, T1 - TH, N])
        zn = sb("zn", [128, RING["N"], MOST["N"], N])
        zs = sb("zs", [128, ZS_RING, MOST["S"], N])
        zh = {k: sb(f"zh_{k}", [128, RING[k], MOST[k], N], F32R) for k in "SD"}
        zl = {k: sb(f"zl_{k}", [128, RING[k], MOST[k], N], F32R) for k in "SD"}
        direct = sb("direct", [128, 3, N])
        zt = sb("zt", [128, 2, B])
        w0a_sb = zn[:, 0, :, :].rearrange("p a (b s) -> p (a b) s", s=S)
        w0b_sb = zn[:, 1, :, :].rearrange("p a (b s) -> p (a b) s", s=S)
        wst = xlo[:, 1, :, :].rearrange("p a (b s) -> p (a b) s", s=S)
        m1 = xlo[:, 0, 0:H1 // 128, :]
        m2 = xlo[:, 0, H1 // 128:(H1 + H2) // 128, :]
        y_sb = xlo[:, 0, (H1 + H2) // 128, 0:B // 128]
        dense_sb = base[0:DC, :]
        wt1_sb = rot[:, 0:3, :]
        wt2_sb = rot[:, 3:5, :].rearrange("p a (b n) -> p (a b) n", n=H2)

        acc = [psum(f"acc{i}", [128, N]) for i in range(3)]
        h_ps = [psum(f"h{i}", [128, N]) for i in range(2)]
        base_ps = psum("base_ps", [128, N])
        zd_ps = psum("zd_ps", [128, MOST["D"], N])
        pm = [acc[0][:, :], base_ps[:, :], zd_ps[:, 0, :], zd_ps[:, 1, :]]
        pm2 = [h_ps[0][:, :], h_ps[1][:, :]]
        py = acc[1][:, 0:B // 128]

        s_ids = sem("s_ids")
        s_idx = sem("s_idx")
        s_w0 = sem("s_w0")
        s_w0zero = sem("s_w0zero")
        s_fold = sem("s_fold")
        s_w1 = sem("s_w1")
        s_w2 = sem("s_w2")
        s_wh = sem("s_wh")
        s_wl = sem("s_wl")
        s_cols = sem("s_cols")
        s_wt = sem("s_wt")
        s_gathered = [sem(f"s_gathered{i}") for i in range(2)]
        s_stored = [sem(f"s_stored{i}") for i in range(2)]
        s_rot = sem("s_rot")
        s_gathered0 = [sem(f"s_gathered0_{i}") for i in range(2)]
        s_stored0 = [sem(f"s_stored0_{i}") for i in range(2)]
        s_rot0 = [sem(f"s_rot0_{i}") for i in range(2)]
        s_base = sem("s_base")
        s_xlo = [sem(f"s_xlo{i}") for i in range(2)]
        s_xhi = sem("s_xhi")
        s_ready = {k: sem(f"s_ready_{k}") for k in "NSD"}
        s_used = {k: sem(f"s_used_{k}") for k in "NSD"}
        s_hi = {k: sem(f"s_hi_{k}") for k in "SD"}
        s_lo = {k: sem(f"s_lo_{k}") for k in "SD"}
        s_hready = [None, sem("s_hready1"), sem("s_hready2")]
        s_evac = [sem(f"s_evac{i}") for i in range(3)]
        s_summed01 = sem("s_summed01")
        s_summed2 = sem("s_summed2")
        s_m1 = sem("s_m1")
        s_m1r = sem("s_m1r")
        s_m2 = sem("s_m2")
        s_m2r = sem("s_m2r")
        s_y = sem("s_y")
        s_yc = sem("s_yc")
        s_out = sem("s_out")

        def done(eng, layer, c, groups):
            kind = PLAN[layer][groups - 1][0]
            k = sum(g[0] == kind for g in PLAN[layer][:groups])
            eng.wait_ge(s_ready[kind], first_group(kind, layer, c) + k)

        block = ctx.enter_context(nc.Block())

        @block.gpsimd
        def _(pool):
            nc.gpsimd.memset(w0b_sb[0:64, 0, :], 0.0).then_inc(s_w0zero, 1)
            pool.wait_ge(s_ids, 16)

            def index(c, slot):
                nc.gpsimd.tensor_tensor(idx_sb[:, slot, :], ids_sb[:, bass.ds(c * NG, NG)], starts_sb,
                                        ALU.add).then_inc(s_idx, 1)

            def gather(slot, js, done=None):
                for j in js:
                    p = 128 if j < NG - 1 else LAST
                    nc.gpsimd.indirect_dma_start(
                        gath[0:p, slot, j, :], None, tables,
                        bass.IndirectOffsetOnAxis(ap=idx_sb[0:p, slot, j:j + 1], axis=0),
                    ).then_inc(done or s_gathered[slot], 16)

            def indexed(c):
                pool.wait_ge(s_idx, c + 1)
                pool.nop(nofuse=True)

            def low(layer, c, par, i):
                number, slot = group_number(layer, c, par, i)
                tiles = PLAN[layer][i][2]
                p = group_rows(layer, i)
                pool.wait_ge(s_hi["S"], number + 1)
                _, z_slot = group_number(layer, c, par, i, ZS_RING)
                nc.gpsimd.tensor_tensor(zl["S"][0:p, slot, 0:tiles, :], zs[0:p, z_slot, 0:tiles, :],
                                        zh["S"][0:p, slot, 0:tiles, :].bitcast(F32),
                                        ALU.subtract).then_inc(s_lo["S"], 1)

            def lows(layer, c, par):
                for i, g in enumerate(PLAN[layer]):
                    if g[0] == "S":
                        low(layer, c, par, i)

            def body(c, slot, stored):
                work = [(l, d, i) for l, d in ((2, 0), (1, 1), (0, 2))
                        for i, g in enumerate(PLAN[l]) if g[0] == "S"]
                for k, (l, d, i) in enumerate(work):
                    low(l, c + d, (1 - slot + d) % 2, i)
                    if stored is not None:
                        if k == 0:
                            pool.wait_ge(s_stored[slot], stored)
                            index(c + 3, slot)
                            indexed(c + 3)
                        gather(slot, range(sum(GATHERS[:k]), sum(GATHERS[:k + 1])))

            index(0, 0)
            indexed(0)
            gather(0, range(WRAP_G), s_gathered0[0])
            gather(0, range(WRAP_G, NG), s_gathered0[1])
            index(1, 1)
            indexed(1)
            gather(1, range(NG))
            pool.wait_ge(s_stored0[0], 32)
            pool.wait_ge(s_stored0[1], 32)
            index(2, 0)
            indexed(2)
            gather(0, range(BEFORE_L0))
            lows(0, 0, 0)
            gather(0, range(BEFORE_L0, NG))
            lows(1, 0, 0)
            lows(0, 1, 1)
            with pool.Fori(0, (CH - 4) // 2) as i:
                for u in range(2):
                    body(i * 2 + u, 1 - u, i * 48 + 48)
            body(CH - 4, 1, 48 * ((CH - 4) // 2 + 1))
            body(CH - 3, 0, None)
            lows(2, CH - 2, 0)
            lows(1, CH - 1, 1)
            lows(2, CH - 1, 1)

        @block.sync
        def _(sp):
            sp.dma_start(ids_sb[:, :], ids).then_inc(s_ids, 16)

            def store(c, slot, n):
                sp.wait_ge(s_gathered[slot], n * (16 * NG))
                g = gath[:, slot, :, :]
                m = (NG - 1) * FG
                sp.dma_start(xt[c, 0:m, :].rearrange("(j q) (b d) -> (q b) j d", q=FG, d=D),
                             g[:, 0:NG - 1, :]).then_inc(s_stored[slot], 16)
                sp.dma_start(xt[c, m:F, :].rearrange("q (b d) -> (q b) d", d=D),
                             g[0:LAST, NG - 1, :]).then_inc(s_stored[slot], 16)
                sp.dma_start(xt[c, F:XROWS, :].rearrange("(j q) (b d) -> (q b) j d", q=FG, d=D),
                             g[:, 0:WRAP_G, :]).then_inc(s_stored[slot], 16)

            def fields(c, first, dims):
                return bass.AP(tensor=xt.tensor, offset=c * (XROWS * N) + first * N,
                               ap=[[n * N, count] for n, count in dims] + [[1, N]])

            def load_base(c, done):
                for j in range(3):
                    sp.dma_start(base[j * F:(j + 1) * F, :], fields(c, 0, [[1, F]])).then_inc(done, 16)

            def load_rot(c, t0, t1, done):
                for j in range(3):
                    tn = min(t1, (R - j + 2) // 3)
                    sp.dma_start(rot[j * F:(j + 1) * F, t0:tn, :],
                                 fields(c, 3 * t0 + j, [[1, F], [3, tn - t0]])).then_inc(done, 16)

            def load_x(c, dst, t0, t1, s):
                for half in range(2):
                    tn = t1 if half == 0 or t1 < T1 else F // 2
                    sp.dma_start(dst[half * G:(half + 1) * G, 0:tn - t0, :],
                                 fields(c, 2 * t0 + half, [[0, G], [2, tn - t0]])).then_inc(s, 16)

            def load_lo(c, slot):
                load_x(c, xlo[:, slot, :, :], 0, TH, s_xlo[slot])

            def load_hi(c):
                load_x(c, xhi[:, :, :], TH, T1, s_xhi)

            def rows(q0, q1):
                return xt[0, q0:q1, :].rearrange("(j q) (b d) -> (q b) j d", q=FG, d=D)

            m = WRAP_G * FG
            sp.wait_ge(s_gathered0[0], 16 * WRAP_G)
            sp.dma_start(rows(0, m), gath[:, 0, 0:WRAP_G, :]).then_inc(s_stored0[0], 16)
            sp.dma_start(rows(F, XROWS), gath[:, 0, 0:WRAP_G, :]).then_inc(s_stored0[0], 16)
            sp.wait_ge(s_gathered0[1], 16 * (NG - WRAP_G))
            sp.dma_start(rows(m, (NG - 1) * FG), gath[:, 0, WRAP_G:NG - 1, :]).then_inc(s_stored0[1], 16)
            sp.dma_start(xt[0, (NG - 1) * FG:F, :].rearrange("q (b d) -> (q b) d", d=D),
                         gath[0:LAST, 0, NG - 1, :]).then_inc(s_stored0[1], 16)
            sp.wait_ge(s_stored0[0], 32)
            sp.wait_ge(s_stored0[1], 32)
            load_base(0, s_rot0[0])
            load_rot(0, 0, ROT_FIRST, s_rot0[0])
            load_rot(0, ROT_FIRST, T0, s_rot0[1])
            load_lo(0, 0)
            load_hi(0)
            store(1, 1, 1)
            sp.wait_ge(s_stored[1], 48)
            done(sp, 0, 0, len(PLAN[0]))
            load_base(1, s_rot)
            load_rot(1, 0, T0, s_rot)
            sp.wait_ge(s_wl, 3)
            load_lo(1, 1)

            with sp.Fori(1, CH // 2) as i:
                for u in range(2):
                    c = i * 2 + u
                    store(c, u, i + u)
                    sp.wait_ge(s_stored[u], (i + u) * 48)
                    done(sp, 0, c - 1, len(PLAN[0]))
                    load_base(c, s_rot)
                    load_rot(c, 0, T0, s_rot)
                    done(sp, 2, c - 2, HALF_DONE[2])
                    load_hi(c - 1)
                    done(sp, 2, c - 2, len(PLAN[2]))
                    load_lo(c, u)
            done(sp, 2, CH - 2, HALF_DONE[2])
            load_hi(CH - 1)
            done(sp, 0, CH - 1, len(PLAN[0]))
            sp.dma_start(wt1_sb[G:128, 0, :], wt1[0:G, :]).then_inc(s_wt, 16)
            sp.dma_start(wt1_sb[0:G, 0, :], wt1[G:2 * G, :]).then_inc(s_wt, 16)
            sp.dma_start(wt1_sb[:, 1, :], wt1[2 * G:ZD, :]).then_inc(s_wt, 16)
            sp.dma_start(wt1_sb[0:DC, 2, :], wt1[ZD:ZD + DC, :]).then_inc(s_wt, 16)
            sp.dma_start(dense_sb, dense).then_inc(s_wt, 16)
            sp.dma_start(wt2_sb, wt2.rearrange("(k p) n -> p k n", p=128)).then_inc(s_wt, 16)
            sp.wait_ge(s_yc, 1)
            sp.dma_start(out.rearrange("(p j) o -> p (j o)", p=128), y_sb).then_inc(s_out, 16)
            sp.wait_ge(s_out, 16)

        @block.vector
        def _(dve):
            dve.wait_ge(s_w0zero, 1)
            dve.wait_ge(s_w0, 80)
            for i, (kind, t0, n) in enumerate(PLAN[0]):
                dst, at = (wn_sb[0], n_weight(0, i)) if kind == "N" else (wst, s_weight(0, i))
                whole = n - (t0 + n == T0)
                if whole:
                    nc.vector.tensor_tensor(dst[0:P0, at:at + whole, :], w0a_sb[0:P0, t0:t0 + whole, :],
                                            w0b_sb[0:P0, t0:t0 + whole, :], ALU.add).then_inc(s_fold, 1)
                if whole < n:
                    nc.vector.tensor_tensor(dst[0:K0_LAST, at + whole, :], w0a_sb[0:K0_LAST, T0 - 1, :],
                                            w0b_sb[0:K0_LAST, T0 - 1, :], ALU.add).then_inc(s_fold, 1)

            def split_weights(l):
                a, b = SPLIT_AT[l:l + 2]
                p = P0 if l == 0 else 128
                dve.wait_ge(s_wh, l + 1)
                nc.vector.tensor_tensor(wl_sb[0:p, a:b, :], wst[0:p, a:b, :], wh_sb[0:p, a:b, :].bitcast(F32),
                                        ALU.subtract).then_inc(s_wl, 1)

            split_weights(0)
            split_weights(1)

            def sum_over_d(dst, src, done):
                nc.vector.tensor_reduce(dst, src.rearrange("p (b d) -> p b d", d=D), AX.X,
                                        ALU.add).then_inc(done, 1)

            def sum01(c, par):
                dve.wait_ge(s_evac[0], c + 1)
                dve.wait_ge(s_evac[1], c + 1)
                sum_over_d(zt[:, 0, bass.ds(c * CB, CB)], direct[:, par, :], s_summed01)

            def sum2(c, n):
                dve.wait_ge(s_evac[2], n)
                sum_over_d(zt[:, 1, bass.ds(c * CB, CB)], direct[:, 2, :], s_summed2)

            def low(layer, c, par, i):
                number, slot = group_number(layer, c, par, i)
                n = PLAN[layer][i][2]
                dve.wait_ge(s_hi["D"], number + 1)
                p = group_rows(layer, i)
                dst = zh["D"][G:128, slot, 0:1, :] if folded(layer, i) else zl["D"][:, slot, 0:n, :]
                nc.vector.tensor_tensor(dst, zd_ps[0:p, 0:n, :], zh["D"][0:p, slot, 0:n, :].bitcast(F32),
                                        ALU.subtract).then_inc(s_lo["D"], 1)

            def x_tiles(layer, par, p, t, n):
                if layer == 0:
                    return rot[0:p, t:t + n, :]
                return xlo[0:p, par, t:t + n, :] if t < TH else xhi[0:p, t - TH:t - TH + n, :]

            def step(layer, c, par):
                for i, (kind, t0, n) in enumerate(PLAN[layer]):
                    number, slot = group_number(layer, c, par, i)
                    if kind == "N" and (not isinstance(number, int) or number >= RING["N"]):
                        dve.wait_ge(s_used["N"], number - (RING["N"] - 1))
                    if kind == "S" and (not isinstance(number, int) or number >= ZS_RING):
                        dve.wait_ge(s_lo["S"], number - (ZS_RING - 1))
                    if kind == "D" and not is_chunk(number, 0):
                        dve.wait_ge(s_lo["D"], number)
                    if layer == 0 and is_chunk(c, 0):
                        if i == 0:
                            dve.wait_ge(s_rot0[0], 96)
                        if t0 + n > ROT_FIRST:
                            dve.wait_ge(s_rot0[1], 48)
                    elif layer == 0 and i == 0:
                        dve.wait_ge(s_rot, c * 96)
                    if layer == 0 and i == 0:
                        dve.wait_ge(s_base, c + 1)
                    if i == 0 and layer > 0:
                        dve.wait_ge(s_hready[layer], c + 1)
                    if i == 0 and layer == 1:
                        dve.wait_ge(s_xlo[par], (c - par) * 16 + 32)
                    if i == HALF_DONE[1] and layer == 1:
                        dve.wait_ge(s_xhi, c * 32 + 32)
                    other = base_ps if layer == 0 else h_ps[layer - 1]
                    p = P0 if layer == 0 else 128
                    if kind == "N":
                        z = zn[:, slot, :, :]
                    else:
                        z_slot = group_number(layer, c, par, i, ZS_RING)[1]
                        z = zs[:, z_slot, :, :] if kind == "S" else zd_ps[:, :, :]
                    ragged = t0 + n == TILES[layer]
                    if n > ragged:
                        m = n - ragged
                        ins = nc.vector.tensor_tensor(
                            z[0:p, 0:m, :], x_tiles(layer, par, p, t0, m),
                            other[0:p, :].unsqueeze(1).broadcast_to([p, m, N]), ALU.mult)
                    if ragged:
                        k = KLAST[layer]
                        ins = nc.vector.tensor_tensor(
                            z[0:k, n - 1, :], x_tiles(layer, par, k, t0 + n - 1, 1)[:, 0, :],
                            other[0:k, :], ALU.mult)
                    ins.then_inc(s_ready[kind], 1)
                    if i > 0 and PLAN[layer][i - 1][0] == "D":
                        low(layer, c, par, i - 1)
                    if layer == 2 and i == 2:
                        sum01(c, par)
                if layer == 0 and is_chunk(c, 0):
                    split_weights(2)
                if layer == 0 and not isinstance(c, int):
                    sum2(c - 2, c - 1)
                if layer == 2 and is_chunk(c, CH - 1):
                    sum2(c - 1, c)

            run_steps(dve, step)
            sum2(CH - 1, CH)
            dve.wait_ge(s_y, 1)
            nc.vector.tensor_copy(y_sb, py).then_inc(s_yc, 1)

        @block.tensor
        def _(pe):
            pe.wait_ge(s_fold, FOLDS)
            pe.wait_ge(s_wl, 1)

            def keep_warm(columns):
                width = SPLIT_AT[1] * S
                for _ in range(columns // width):
                    nc.tensor.matmul(acc[2][:, 0:width], wh_sb[0:P0, 0, :],
                                     wh_sb[0:P0, 0:SPLIT_AT[1], :].rearrange("p a s -> p (a s)"),
                                     start=True, stop=True)

            def mlp_early():
                pe.wait_ge(s_wt, 16 * 6)
                pe.wait_ge(s_summed01, CH - 1)
                pe.wait_ge(s_evac[0], CH)
                for m in range(EARLY_M):
                    ms = slice(m * 128, (m + 1) * 128)
                    nc.tensor.matmul(pm[m], wt1_sb[0:DC, 2, ms], dense_sb, start=True, stop=False)
                    nc.tensor.matmul(pm[m][:, 0:EARLY], wt1_sb[:, 0, ms], zt[:, 0, 0:EARLY],
                                     start=False, stop=False)

            pe.wait_ge(s_stored0[1], 32)
            keep_warm(WARM0)

            def step(layer, c, par):
                if is_chunk(c, 0) and layer == 1:
                    pe.wait_ge(s_w1, W_LOADS[1] * 16)
                    pe.wait_ge(s_wl, 3)
                    keep_warm(WARM1)
                if layer == 0 and is_chunk(c, 1):
                    pe.wait_ge(s_w2, W_LOADS[2] * 16)
                if layer < 2 and not is_chunk(c, 0):
                    pe.wait_ge(s_evac[layer], c)
                if layer == 0 and not isinstance(c, int):
                    pe.wait_ge(s_evac[2], c - 1)
                if layer == 2 and is_chunk(c, CH - 1):
                    mlp_early()
                    pe.wait_ge(s_evac[2], c)
                out_ps = acc[layer][:, :]
                for o, i in enumerate(PE_ORDER[layer]):
                    kind, t0, n = PLAN[layer][i]
                    number, slot = group_number(layer, c, par, i)
                    pe.wait_ge(s_ready["N"] if kind == "N" else s_lo[kind], number + 1)
                    for k in range(n):
                        t = t0 + k
                        p = (P0 if layer == 0 else 128) if t < TILES[layer] - 1 else KLAST[layer]
                        first, last = o == 0 and k == 0, o == len(PLAN[layer]) - 1 and k == n - 1
                        if kind == "N":
                            mm = nc.tensor.matmul(out_ps, wn_sb[layer][0:p, n_weight(layer, i) + k, :],
                                                  zn[0:p, slot, k, :], start=first, stop=last)
                        else:
                            a = s_weight(layer, i) + k
                            wh, wl, high = wh_sb[0:p, a, :], wl_sb[0:p, a, :], zh[kind][0:p, slot, k, :]
                            nc.tensor.matmul(out_ps, wl, high, start=first, stop=False)
                            if folded(layer, i):
                                mm = nc.tensor.matmul(out_ps, wh_sb[:, a, :], zh[kind][:, slot, k, :],
                                                      start=False, stop=last)
                            else:
                                nc.tensor.matmul(out_ps, wh, zl[kind][0:p, slot, k, :], start=False, stop=False)
                                mm = nc.tensor.matmul(out_ps, wh, high, start=False, stop=last)
                    mm.then_inc(s_used[kind], 1)

            run_steps(pe, step)

            pe.wait_ge(s_summed01, CH)
            for m in range(H1 // 128):
                ms = slice(m * 128, (m + 1) * 128)
                if m < EARLY_M:
                    nc.tensor.matmul(pm[m][:, EARLY:B], wt1_sb[:, 0, ms], zt[:, 0, EARLY:B],
                                     start=False, stop=False)
                else:
                    nc.tensor.matmul(pm[m], wt1_sb[0:DC, 2, ms], dense_sb, start=True, stop=False)
                    nc.tensor.matmul(pm[m], wt1_sb[:, 0, ms], zt[:, 0, :], start=False, stop=False)
            pe.wait_ge(s_summed2, CH)
            for m in range(H1 // 128):
                nc.tensor.matmul(pm[m], wt1_sb[:, 1, m * 128:(m + 1) * 128], zt[:, 1, :],
                                 start=False, stop=True).then_inc(s_m1, 1)
            for k in range(H1 // 128):
                pe.wait_ge(s_m1r, k + 1)
                for m in range(H2 // 128):
                    mm = nc.tensor.matmul(pm2[m], wt2_sb[:, k, m * 128:(m + 1) * 128], m1[:, k, :],
                                          start=(k == 0), stop=(k == H1 // 128 - 1))
                    if k == H1 // 128 - 1:
                        mm.then_inc(s_m2, 1)
            pe.wait_ge(s_m2r, H2 // 128)
            for j in range(B // 128):
                for k in range(H2 // 128):
                    rows = m2[:, k, :].rearrange("q (p j) -> q j p", p=128)[:, j, :]
                    mm = nc.tensor.matmul(py[:, j:j + 1], rows, wt3_sb[:, k:k + 1], start=(k == 0),
                                          stop=(k == H2 // 128 - 1))
            mm.then_inc(s_y, 1)

        @block.scalar
        def _(act):
            act.dma_start(w0a_sb[0:P0, 0:T0 - 1, :], w0a[0:P0 * (T0 - 1), :].rearrange("(t p) s -> p t s", p=P0)
                          ).then_inc(s_w0, 16)
            act.dma_start(w0a_sb[0:K0_LAST, T0 - 1, :], w0a[P0 * (T0 - 1):, :]).then_inc(s_w0, 16)
            act.wait_ge(s_w0zero, 1)
            act.dma_start(w0b_sb[F:P0, 0, :], w0b[0:2 * F, :]).then_inc(s_w0, 16)
            act.dma_start(w0b_sb[0:P0, 1:T0 - 1, :],
                          w0b[2 * F:2 * F + P0 * (T0 - 2), :].rearrange("(t p) s -> p t s", p=P0)
                          ).then_inc(s_w0, 16)
            act.dma_start(w0b_sb[0:K0_LAST, T0 - 1, :], w0b[2 * F + P0 * (T0 - 2):, :]).then_inc(s_w0, 16)
            act.dma_start(cols_sb[:, :], cols).then_inc(s_cols, 16)

            def load_weights(l, w, done):
                for i, (kind, t0, n) in enumerate(PLAN[l]):
                    dst, at = (wn_sb[l], n_weight(l, i)) if kind == "N" else (wst, s_weight(l, i))
                    whole = n - (t0 + n == T1)
                    if whole:
                        act.dma_start(dst[:, at:at + whole, :],
                                      w[t0 * 128:(t0 + whole) * 128, :].rearrange("(t p) s -> p t s", p=128)
                                      ).then_inc(done, 16)
                    if whole < n:
                        act.dma_start(dst[0:K1_LAST, at + whole, :], w[(T1 - 1) * 128:, :]).then_inc(done, 16)
                    if folded(l, i):
                        act.dma_start(dst[G:128, at, :], w[(T1 - 1) * 128:, :]).then_inc(done, 16)

            def round_weights(l):
                a, b = SPLIT_AT[l:l + 2]
                p = P0 if l == 0 else 128
                nc.scalar.copy(wh_sb[0:p, a:b, :], wst[0:p, a:b, :]).then_inc(s_wh, 1)

            load_weights(1, w1, s_w1)
            act.wait_ge(s_fold, FOLDS)
            round_weights(0)
            act.wait_ge(s_w1, W_LOADS[1] * 16)
            round_weights(1)
            load_weights(2, w2, s_w2)
            act.wait_ge(s_cols, 16)

            def high(layer, c, par, groups):
                for i in groups:
                    kind, _, n = PLAN[layer][i]
                    p = group_rows(layer, i)
                    number, slot = group_number(layer, c, par, i)
                    act.wait_ge(s_ready[kind], number + 1)
                    if not isinstance(number, int) or number >= RING[kind]:
                        act.wait_ge(s_used[kind], number - (RING[kind] - 1))
                    z_slot = group_number(layer, c, par, i, ZS_RING)[1]
                    z = zs[0:p, z_slot, 0:n, :] if kind == "S" else zd_ps[0:p, 0:n, :]
                    nc.scalar.copy(zh[kind][0:p, slot, 0:n, :], z).then_inc(s_hi[kind], 1)

            def copy_base(c):
                if is_chunk(c, 0):
                    act.wait_ge(s_rot0[0], 96)
                else:
                    act.wait_ge(s_rot, c * 96)
                    done(act, 0, c - 1, len(PLAN[0]))
                nc.scalar.copy(base_ps[0:P0, :], base[0:P0, :]).then_inc(s_base, 1)

            def finish(layer, c, par):
                kind = PLAN[layer][PE_ORDER[layer][-1]][0]
                act.wait_ge(s_used[kind], first_group(kind, layer, c) + PER_LAYER[kind][layer])
                if layer < 2:
                    nc.scalar.activation(h_ps[layer][0:G, :], acc[layer][0:G, :], ACT.Relu,
                                         bias=bias[0:G, layer:layer + 1])
                    nc.scalar.activation(h_ps[layer][G:128, :], acc[layer][0:G, :], ACT.Relu,
                                         bias=bias[0:G, layer:layer + 1]).then_inc(s_hready[layer + 1], 1)
                    dst = direct[G:128, par, :] if layer == 0 else direct[0:G, par, :]
                    nc.scalar.activation(dst, acc[layer][G:128, :], ACT.Relu,
                                         bias=bias[G:128, layer:layer + 1]).then_inc(s_evac[layer], 1)
                else:
                    if is_chunk(c, CH - 1):
                        act.wait_ge(s_summed2, c)
                    nc.scalar.activation(direct[:, 2, :], acc[2][:, :], ACT.Relu,
                                         bias=bias[:, 2:3]).then_inc(s_evac[2], 1)

            def step(layer, c, par):
                s_at = [i for i, g in enumerate(PLAN[layer]) if g[0] != "N"]
                at = FINISH_AT[layer]
                if layer == 0:
                    if isinstance(c, int):
                        copy_base(c)
                    high(0, c, par, s_at[:at])
                    if is_chunk(c, 0):
                        act.wait_ge(s_w2, W_LOADS[2] * 16)
                        round_weights(2)
                    if not is_chunk(c, 0):
                        finish(1, c - 1, 1 - par)
                    high(0, c, par, s_at[at:])
                elif layer == 1:
                    if is_chunk(c, 0):
                        finish(0, c, par)
                        high(1, c, par, s_at)
                    else:
                        high(1, c, par, s_at[:at])
                        finish(2, c - 1, 1 - par)
                        if not is_chunk(c, CH - 1):
                            copy_base(c + 1)
                        high(1, c, par, s_at[at:])
                else:
                    if is_chunk(c, CH - 1):
                        finish(1, c, par)
                        high(2, c, par, s_at)
                        finish(2, c, par)
                    else:
                        high(2, c, par, s_at[:at])
                        finish(0, c + 1, 1 - par)
                        high(2, c, par, s_at[at:])

            run_steps(act, step)
            for m in range(H1 // 128):
                act.wait_ge(s_m1, m + 1)
                nc.scalar.activation(m1[:, m, :], pm[m], ACT.Relu, bias=bt1_sb[:, m:m + 1]).then_inc(s_m1r, 1)
            for m in range(H2 // 128):
                act.wait_ge(s_m2, m + 1)
                nc.scalar.activation(m2[:, m, :], pm2[m], ACT.Relu, bias=bt2_sb[:, m:m + 1]).then_inc(s_m2r, 1)


def kernel(**inputs):
    import concourse.bacc as bacc
    from concourse.bass_utils import run_bass_kernel_spmd

    tables = [np.asarray(inputs[f"tbl_{f}"]) for f in range(F)]
    starts = np.cumsum([0] + [t.shape[0] for t in tables[:-1]]).astype(np.int32)
    ids = np.zeros((NG * FG, B), np.int32)
    ids[0:F] = np.asarray(inputs["ids"]).T
    starts_of = np.zeros((NG * FG, B), np.int32)
    starts_of[0:F] = starts[:, None]

    def spread(a):
        return np.ascontiguousarray(a.reshape(NG, FG, CH, CB).transpose(1, 3, 2, 0).reshape(128, CH * NG))

    g = np.arange(F)
    w0 = np.asarray(inputs["L0_rec_W0"]).reshape(F, F, S)
    w0a = np.concatenate([w0[g, (g + r) % F] for r in range(R)])
    w0b = np.concatenate([w0[(g + r) % F, g] for r in range(1, R)])
    arrays = {
        "tables": np.concatenate(tables),
        "ids": np.concatenate([spread(ids), spread(starts_of)[:, 0:NG]], axis=1),
        "dense": np.ascontiguousarray(np.asarray(inputs["dense_ctx"]).T),
        "w0a": w0a, "w0b": w0b,
        "w1": np.asarray(inputs["L0_rec_W1"]), "w2": np.asarray(inputs["L0_rec_W2"]),
        "wt1": np.asarray(inputs["W_top1"]), "wt2": np.asarray(inputs["W_top2"]),
        "cols": np.ascontiguousarray(np.concatenate(
            [np.asarray(inputs[n]).reshape(-1, 128) for n in
             ("L0_rec_b0", "L0_rec_b1", "L0_rec_b2", "b_top1", "b_top2", "W_top3")]).T),
    }
    nc = bacc.Bacc("TRN2", target_bir_lowering=False, num_devices=1,
                   dynamic_dma_scratch_size=SCRATCH)
    args = [nc.dram_tensor(n, a.shape, mybir.dt.from_np(a.dtype), kind="ExternalInput").ap()
            for n, a in arrays.items()]
    out = nc.dram_tensor("out", (B, 1), F32, kind="ExternalOutput").ap()
    build(nc, *args, out)
    return run_bass_kernel_spmd(nc, [arrays], core_ids=[0]).results[0]["out"]
```
